# Optimizing a Trainium2 kernel written in Bass

```python
import numpy as np
import jax
import jax.numpy as jnp

def _softmax(x, axis=-1):
    return jax.nn.softmax(x, axis=axis)

def _gelu(x):
    return jax.nn.gelu(x, approximate=True)

def _silu(x):
    return jax.nn.silu(x)

def _sigmoid(x):
    return jax.nn.sigmoid(x)

def _layernorm(x, axis=-1, eps=1e-05):
    m = jnp.mean(x, axis=axis, keepdims=True)
    v = jnp.var(x, axis=axis, keepdims=True)
    return (x - m) / jnp.sqrt(v + eps)

def _scatter_add(tgt, idx, src, axis=0):
    return tgt.at[idx].add(src)

def _segment_sum(src, seg, n):
    return jax.ops.segment_sum(src, seg, n)
kernel_name = 'mk_cond_resid_d1_seqx_r4_3c967f'

def setup_inputs(seed: int=0):
    np.random.seed(seed)
    _w = jnp.asarray

    def _rec_inputs():
        import jax
        import jax.numpy as jnp
        _rk = jax.random.key(seed)
        x = -0.0003929 + 0.9999 * jax.random.normal(jax.random.fold_in(_rk, 1), (8, 512, 256), jnp.float32)
        _lenS = 512 - jax.random.randint(jax.random.fold_in(_rk, 7), (8,), 0, max(1, 512 // 4) + 1, jnp.int32)
        _lenS2 = 512 - jax.random.randint(jax.random.fold_in(_rk, 8), (8,), 0, max(1, 512 // 4) + 1, jnp.int32)
        cond_2048 = 0.00782532 + 1.00527 * jax.random.normal(jax.random.fold_in(_rk, 11), (8, 512), jnp.float32)
        return (x, cond_2048)
    x, cond_2048 = _rec_inputs()

    def _L0_cond_setup():
        import jax, jax.numpy as jnp
        import numpy as np
        B, S, D_MODEL, D_INNER, D_STATE = (4, 1024, 256, 512, 16)
        key = jax.random.key(seed)
        ks = jax.random.split(key, 12)
        inp = {'x': jax.random.normal(ks[0], (B, S, D_MODEL), jnp.float32), 't_emb': jax.random.normal(ks[1], (B, D_INNER), jnp.float32), 'W_in': jax.random.normal(ks[2], (2 * D_INNER, D_MODEL), jnp.float32) * 0.02, 'W_conv': jax.random.normal(ks[3], (D_INNER, 1, 4), jnp.float32) * 0.1, 'b_conv': jnp.zeros((D_INNER,), jnp.float32), 'ln_g': jnp.ones((D_INNER,), jnp.float32), 'ln_b': jnp.zeros((D_INNER,), jnp.float32), 'W_xproj': jax.random.normal(ks[4], (3 * D_STATE, D_INNER), jnp.float32) * 0.02, 'W_dt': jax.random.normal(ks[5], (D_STATE, D_STATE), jnp.float32) * 0.01, 'b_dt': jax.random.uniform(ks[6], (D_STATE,), jnp.float32) * 0.1, 'A_log': jax.random.normal(ks[7], (D_STATE,), jnp.float32) * 0.1, 'D': jnp.ones((D_INNER,), jnp.float32) * 0.1, 'W_out': jax.random.normal(ks[8], (D_MODEL, D_INNER), jnp.float32) * 0.02}
        return inp
    _L0_cond_all = _L0_cond_setup()
    _L0_cond_in = {k: v for k, v in _L0_cond_all.items() if k in ('W_in', 'W_conv', 'b_conv', 'ln_g', 'ln_b', 'W_xproj', 'W_dt', 'b_dt', 'A_log', 'D', 'W_out')}
    del _L0_cond_all
    return {'x': x, 'cond_2048': cond_2048, 'L0_cond_W_in': _L0_cond_in['W_in'], 'L0_cond_W_conv': _L0_cond_in['W_conv'], 'L0_cond_b_conv': _L0_cond_in['b_conv'], 'L0_cond_ln_g': _L0_cond_in['ln_g'], 'L0_cond_ln_b': _L0_cond_in['ln_b'], 'L0_cond_W_xproj': _L0_cond_in['W_xproj'], 'L0_cond_W_dt': _L0_cond_in['W_dt'], 'L0_cond_b_dt': _L0_cond_in['b_dt'], 'L0_cond_A_log': _L0_cond_in['A_log'], 'L0_cond_D': _L0_cond_in['D'], 'L0_cond_W_out': _L0_cond_in['W_out']}

def reference(x, cond_2048, L0_cond_W_in, L0_cond_W_conv, L0_cond_b_conv, L0_cond_ln_g, L0_cond_ln_b, L0_cond_W_xproj, L0_cond_W_dt, L0_cond_b_dt, L0_cond_A_log, L0_cond_D, L0_cond_W_out):
    import jax
    import jax.numpy as jnp

    def _L0_cond_ref(x, t_emb, W_in, W_conv, b_conv, ln_g, ln_b, W_xproj, W_dt, b_dt, A_log, D, W_out):
        import jax, jax.numpy as jnp
        import numpy as np
        B, S, D_MODEL, D_INNER, D_STATE = (4, 1024, 256, 512, 16)
        d_inner = W_conv.shape[0]
        d_state = A_log.shape[0]
        xr, gate = jnp.split(x @ W_in.T, 2, axis=-1)
        xr = xr + t_emb[:, None, :]
        xc = jax.lax.conv_general_dilated(xr.transpose(0, 2, 1), W_conv, (1,), [(3, 0)], feature_group_count=d_inner, dimension_numbers=('NCH', 'OIH', 'NCH')) + b_conv[None, :, None]
        xc = jax.nn.silu(xc).transpose(0, 2, 1)
        mu = xc.mean(-1, keepdims=True)
        var = xc.var(-1, keepdims=True)
        xn = (xc - mu) / jnp.sqrt(var + 1e-05) * ln_g + ln_b
        Bm, Cm, dt = jnp.split(xn @ W_xproj.T, 3, axis=-1)
        dt = jnp.tanh(dt @ W_dt.T + b_dt) * 0.01
        A = -jnp.tanh(A_log)
        Ad = 1.0 + dt * A
        Bd = Bm * jnp.minimum(jnp.linalg.norm(xn, axis=-1, keepdims=True), 1.0)
        h0 = jnp.zeros((xn.shape[0], d_state, d_inner), xn.dtype)

        def step(h, inputs):
            ad, bd, xt, ct = inputs
            h = jnp.clip(h * ad[:, :, None] + bd[:, :, None] * xt[:, None, :], -10.0, 10.0)
            yt = jnp.einsum('bd,bdh->bh', ct, h)
            return (h, yt)
        _, ys = jax.lax.scan(step, h0, (Ad.transpose(1, 0, 2), Bd.transpose(1, 0, 2), xn.transpose(1, 0, 2), Cm.transpose(1, 0, 2)))
        y = ys.transpose(1, 0, 2) + D * xn
        return y * jax.nn.silu(gate) @ W_out.T
    x = x + _L0_cond_ref(x, cond_2048, L0_cond_W_in, L0_cond_W_conv, L0_cond_b_conv, L0_cond_ln_g, L0_cond_ln_b, L0_cond_W_xproj, L0_cond_W_dt, L0_cond_b_dt, L0_cond_A_log, L0_cond_D, L0_cond_W_out)
    return x

_drawn_inputs = setup_inputs


def setup_inputs(seed=0):
    import zlib

    import numpy as np

    out = dict(_drawn_inputs(seed))
    spreads = {'L0_cond_b_conv': (0.0, 0.1),
     'L0_cond_ln_g': (1.0, 0.2),
     'L0_cond_ln_b': (0.0, 0.1),
     'L0_cond_D': (0.10000000149011612, 0.6)}
    factors = {'L0_cond_W_dt': 30.012, 'L0_cond_b_dt': 8.0, 'L0_cond_A_log': 8.0}
    for name, (base, spread) in spreads.items():
        noise = np.random.default_rng([zlib.crc32(name.encode()), seed]).standard_normal(out[name].shape)
        drawn = base * np.exp(spread * noise) if base else spread * noise
        out[name] = jnp.asarray(drawn.astype(out[name].dtype))
    for name, factor in factors.items():
        out[name] = (out[name] * factor).astype(out[name].dtype)
    return out
```

```python
from contextlib import ExitStack

import numpy as np

import concourse.bass as bass
from concourse import mybir

F32 = mybir.dt.float32
BF16 = mybir.dt.bfloat16
ALU = mybir.AluOpType
ACT = mybir.ActivationFunctionType

NB, SEQ, DM = 8, 512, 256
DI, NS = 512, 16
T = 16
NCH = SEQ // T
TAPS = 4
MT, KT = DI // 128, DM // 128
HIST = (TAPS - 1) * NB
CLIP = 10.0
XPART = (0, 0, 0, 1, 1, 2)
BPART = (0, 1, 2, 0, 1, 0)
NJ = len(XPART)
KV = NJ * NB
AHEAD = 3
MAIN = range(2, 14)


def from_chunk(i, k, first):
    return not isinstance(i, int) or 2 * i + k >= first


def ready_values(eng, *values):
    for value in values:
        if not isinstance(value, int):
            eng.compute_val(value)
    return values


def place(s):
    q, r = s % 4, s // 4
    return 8 * (q % 2) + 2 * r + q // 2


def bcast(ap, axis, n):
    ap = ap.unsqueeze(axis)
    shape = list(ap.shape)
    shape[axis] = n
    return ap.to_broadcast(shape)


def build(nc, d):
    with ExitStack() as ctx:
        def sb(name, shape, dt=F32):
            return ctx.enter_context(nc.sbuf_tensor(name, shape, dt))

        def psum(name):
            return ctx.enter_context(nc.psum_tensor(name, [128, 512], F32))

        def sem(name):
            return ctx.enter_context(nc.semaphore(name))

        xn_dram = nc.dram_tensor("xn_scratch", (NCH, 128, DI), F32, kind="Internal").ap()
        xp_dram = nc.dram_tensor("xp_scratch", (3, NCH, 128, DI), BF16, kind="Internal").ap()

        win = sb("win", [128, KT, 2 * DI])
        wout = sb("wout", [128, MT, DM])
        wx = sb("wx", [128, MT, 3 * NS])
        wxdt = sb("wxdt", [NS, DI])
        wdt = sb("wdt", [NS, NS])
        cond = sb("cond", [NB, DI])
        ind8 = sb("ind8", [NB, 128])
        wconv = sb("wconv", [128, MT, TAPS])
        bconv = sb("bconv", [128, MT])
        gain = sb("gain", [128, DI])
        beta = sb("beta", [128, DI])
        dskip = sb("dskip", [128, DI])
        alog = sb("alog", [128, 1])
        acol = sb("acol", [128, 1])
        bdt = sb("bdt", [128, 1])
        ident = sb("ident", [128, 128])
        identb = sb("identb", [128, 128], BF16)
        rowmask = sb("rowmask", [128, NB])
        tokmask = sb("tokmask", [128, NB])
        tsel = sb("tsel", [128, T])
        expo = sb("expo", [128, 2])

        xt = [sb(f"xt{j}", [128, KT, 128]) for j in range(2)]
        xrb = [sb(f"xrb{j}", [128, MT, HIST + 128]) for j in range(2)]
        conv = sb("conv", [128, MT, 128])
        tap = [sb(f"tap{n}", [128, MT, 128]) for n in range(TAPS)]
        xc = [sb(f"xc{j}", [128, MT, 128]) for j in range(2)]
        stats = sb("stats", [128, 6])
        mv = sb("mv", [128, 2])
        vare = sb("vare", [128, 1])
        rstd = sb("rstd", [128, 1])
        nmr = sb("nmr", [128, 1])
        xhat = sb("xhat", [128, DI])
        xg = sb("xg", [128, DI])
        xn = [sb(f"xn{j}", [128, DI]) for j in range(2)]
        sq = sb("sq", [128, DI])
        ss = [sb(f"ss{j}", [128, 1]) for j in range(2)]
        res = sb("res", [128, DI])
        xp = [[sb(f"xp{p}_{j}", [128, DI], BF16) for j in range(2)] for p in range(3)]
        xnT = sb("xnT", [128, MT, 128])
        sscap = sb("sscap", [128, 1])
        ncap = sb("ncap", [128, 1])
        zs = sb("zs", [128, 3 * NS])
        zx = sb("zx", [128, 3, NB, NS])
        th = sb("th", [128, T])
        bc = sb("bc", [128, 2, T])
        bres = sb("bres", [128, T])
        bp = [sb(f"bp{p}", [128, T], BF16) for p in range(3)]
        spread = sb("spread", [128, T, 64], BF16)
        ad = [sb(f"ad{j}", [128, T]) for j in range(2)]
        vw = [sb(f"vw{j}", [128, T // 2, 128], BF16) for j in range(2)]
        cw = [sb(f"cw{j}", [128, 4, 136]) for j in range(2)]
        xr = [sb(f"xr{j}", [128, T // 2, DI], BF16) for j in range(2)]
        pre = sb("pre", [128, DI])
        h = sb("h", [128, 8, DI])
        xtb = [sb(f"xtb{j}", [128, KT, 128]) for j in range(2)]
        xres = [sb(f"xres{j}", [128, DM]) for j in range(2)]
        xnb = [sb(f"xnb{j}", [128, DI]) for j in range(2)]
        dxn = sb("dxn", [128, DI])
        sg = sb("sg", [128, DI])
        y1 = sb("y1", [128, DI])
        yg = sb("yg", [128, DI])
        ygT = sb("ygT", [128, MT, 128])
        fin = [sb(f"fin{j}", [128, DM]) for j in range(2)]

        pv = [psum(f"pv{j}") for j in range(4)]
        py = psum("py")
        pa = psum("pa")
        pb = psum("pb")
        pg = psum("pg")
        pab = pa[:, :].bitcast(BF16)
        Z, BLK, OUT = slice(0, 48), 64, slice(256, 512)

        s_const = sem("s_const")
        s_zero = sem("s_zero")
        s_wdt = sem("s_wdt")
        s_wx = sem("s_wx")
        s_acol = sem("s_acol")
        s_idb = sem("s_idb")
        s_xt = [sem(f"s_xt{j}") for j in range(2)]
        s_xr = sem("s_xr")
        s_xrb = sem("s_xrb")
        s_tap = sem("s_tap")
        s_cv = sem("s_cv")
        s_xc = sem("s_xc")
        s_xct = sem("s_xct")
        s_st = sem("s_st")
        s_vare = sem("s_vare")
        s_rstd = sem("s_rstd")
        s_nmr = sem("s_nmr")
        s_xhat = sem("s_xhat")
        s_xg = sem("s_xg")
        s_xn = sem("s_xn")
        s_ss = sem("s_ss")
        s_x1 = sem("s_x1")
        s_r1 = sem("s_r1")
        s_x2 = sem("s_x2")
        s_x3 = sem("s_x3")
        s_scr = [sem(f"s_scr{j}") for j in range(2)]
        s_xp = [sem(f"s_xp{j}") for j in range(2)]
        s_xnt = sem("s_xnt")
        s_xnts = sem("s_xnts")
        s_cap = sem("s_cap")
        s_ncap = sem("s_ncap")
        s_z = sem("s_z")
        s_zb = sem("s_zb")
        s_zc = sem("s_zc")
        s_zx = sem("s_zx")
        s_blk = sem("s_blk")
        s_th = sem("s_th")
        s_bc = sem("s_bc")
        s_ad = sem("s_ad")
        s_bp = sem("s_bp")
        s_sp = sem("s_sp")
        s_cw = sem("s_cw")
        s_vt = sem("s_vt")
        s_vw = sem("s_vw")
        s_v = sem("s_v")
        s_pre = sem("s_pre")
        s_h = sem("s_h")
        s_yg = sem("s_yg")
        s_bk = [sem(f"s_bk{j}") for j in range(2)]
        s_gate = sem("s_gate")
        s_sg = sem("s_sg")
        s_dxn = sem("s_dxn")
        s_y1 = sem("s_y1")
        s_ygs = sem("s_ygs")
        s_yt = sem("s_yt")
        s_yts = sem("s_yts")
        s_o = sem("s_o")
        s_fin = sem("s_fin")
        s_out = [sem(f"s_out{j}") for j in range(2)]

        consts = [(win[:, :, :], d["w_in"]), (wout[:, :, :], d["w_out"]), (wx[:, :, :], d["w_xp"]),
                  (wxdt[:, :], d["w_xdt"]), (wdt[:, :], d["w_dt"]), (cond[:, :], d["cond"]),
                  (ind8[:, :], d["ind8"]), (wconv[:, :, :], d["w_conv"]), (bconv[:, :], d["b_conv"]),
                  (gain[:, :], d["gain"]), (beta[:, :], d["beta"]), (dskip[:, :], d["dskip"]),
                  (alog[:, :], d["alog"]), (bdt[:, :], d["b_dt"]), (ident[:, :], d["ident"]),
                  (rowmask[:, :], d["rowmask"]), (tokmask[:, :], d["tokmask"]), (tsel[:, :], d["tsel"]),
                  (expo[:, :], d["expo"])]
        CONST = 16 * len(consts)
        READY = (s_const, CONST)

        def num(i, k, per=1, more=0):
            return i * (2 * per) + (per * k + more)

        def turn(i, k, per=1, more=0):
            return i * per + (per * (k // 2) + more)

        def stage(i, k, ahead):
            return min(2 * i + k + ahead, NCH) if isinstance(i, int) else num(i, k, 1, ahead)

        block = ctx.enter_context(nc.Block())

        @block.sync
        def _(sp):
            def load_xt(i, k):
                if from_chunk(i, k, 2):
                    read, = ready_values(sp, num(i, k, 1, -1))
                    sp.wait_ge(*READY)
                    sp.wait_ge(s_xr, read)
                sp.dma_start(xt[k % 2][:, :, :], d["xT"][bass.ds(num(i, k), 1)].rearrange("o p k n -> (o p) k n")
                             ).then_inc(s_xt[k % 2], 16)

            def store_scratch(i, k):
                j = k % 2
                made, = ready_values(sp, num(i, k, 1, 1))
                sp.wait_ge(*READY)
                sp.wait_ge(s_xn, made)
                sp.dma_start(xn_dram[bass.ds(num(i, k), 1)].rearrange("o p n -> (o p) n"), xn[j][:, :]).then_inc(s_scr[j], 16)
                for p, ready in enumerate((s_x1, s_x2, s_x3)):
                    made, = ready_values(sp, num(i, k, 1, 1))
                    sp.wait_ge(*READY)
                    sp.wait_ge(ready, made)
                    sp.dma_start(xp_dram[p][bass.ds(num(i, k), 1)].rearrange("o p n -> (o p) n"), xp[p][j][:, :]
                                 ).then_inc(s_scr[j], 16)

            def load_xr(i, k):
                j = k % 2
                stored, read = ready_values(sp, turn(i, k, 64, 64), num(i, k, T, -T))
                sp.wait_ge(*READY)
                sp.wait_ge(s_scr[j], stored)
                if from_chunk(i, k, 2):
                    sp.wait_ge(s_v, read)
                for n, p in enumerate(XPART):
                    for e in range(2):
                        row = 64 * e + NB * n
                        sp.dma_start(xr[j][row:row + NB, :, :], xp_dram[p][bass.ds(num(i, k), 1), 64 * e:64 * e + 64]
                                     .rearrange("o (f b) n -> (o b) f n", b=NB)
                                     ).then_inc(s_xp[j], 16)

            def load_back(i, k):
                j = k % 2
                stored, read = ready_values(sp, turn(i, k, 64, 64), num(i, k, 1, -1))
                sp.wait_ge(*READY)
                sp.wait_ge(s_scr[j], stored)
                if from_chunk(i, k, 2):
                    sp.wait_ge(s_dxn, read)
                    sp.wait_ge(s_gate, read)
                    sp.wait_ge(s_fin, read)
                c = bass.ds(num(i, k), 1)
                sp.dma_start(xnb[j][:, :], xn_dram[c].rearrange("o p n -> (o p) n")).then_inc(s_bk[j], 16)
                sp.dma_start(xtb[j][:, :, :], d["xT"][c].rearrange("o p k n -> (o p) k n")).then_inc(s_bk[j], 16)
                sp.dma_start(xres[j][:, :], d["x"][c].rearrange("o p n -> (o p) n")).then_inc(s_bk[j], 16)

            def store_out(i, k):
                made, = ready_values(sp, num(i, k, 1, 1))
                sp.wait_ge(*READY)
                sp.wait_ge(s_fin, made)
                sp.dma_start(d["out"][bass.ds(num(i, k), 1)].rearrange("o p n -> (o p) n"), fin[k % 2][:, :]
                             ).then_inc(s_out[k % 2], 16)

            def pair(i, fixed=None):
                for k in range(2):
                    c = 4 if fixed is None else 2 * fixed + k
                    if c >= 2:
                        store_out(i, k - 2)
                    load_back(i, k)
                    if c + 1 < NCH:
                        load_xr(i, k + 1)
                    if c + 4 < NCH:
                        load_xt(i, k + 4)
                    if c + 2 < NCH:
                        store_scratch(i, k + 2)

            for dst, src in consts:
                sp.dma_start(dst, src).then_inc(s_const, 16)
            load_xt(0, 0)
            load_xt(0, 1)
            load_xt(0, 2)
            store_scratch(0, 0)
            load_xr(0, 0)
            load_xt(0, 3)
            store_scratch(0, 1)
            pair(0, 0)
            pair(1, 1)
            with sp.Fori(MAIN.start, MAIN.stop) as i:
                pair(i)
            pair(14, 14)
            pair(15, 15)
            store_out(15, 0)
            store_out(15, 1)
            for j in range(2):
                sp.wait_ge(s_out[j], 16 * NCH // 2)

        @block.tensor
        def _(pe):
            def step_product(i, k, s):
                j, slot, row = k % 2, place(s) // 2, 64 * (place(s) % 2)
                if s == 0:
                    pe.wait_ge(s_vw, num(i, k, 1, 1))
                    pe.wait_ge(s_xp[j], turn(i, k, 192, 192))
                if s >= 4 or from_chunk(i, k, 1):
                    pe.wait_ge(s_pre, num(i, k, T, s - 3))
                pe.matmul(pv[s % 4][:, :], vw[j][row:row + KV, slot, :], xr[j][row:row + KV, slot, :],
                          start=True, stop=True).then_inc(s_v, 1)

            def y_group(i, k, r):
                if r == 0:
                    pe.wait_ge(s_cw, num(i, k, 1, 1))
                    if from_chunk(i, k, 1):
                        pe.wait_ge(s_y1, num(i, k))
                pe.wait_ge(s_h, num(i, k, T, 4 * r + 4))
                for q in range(4):
                    mm = pe.matmul(py[32 * q:32 * q + 32, :], c_of(k % 2)[:, 128 * r + 32 * q:128 * r + 32 * q + 32],
                                   h[:, (4 * r + q) % 8, :], start=(r == 0), stop=(r == 3),
                                   tile_position=(0, 32 * q))
                mm.then_inc(s_yg, 1)

            def c_of(j):
                return cw[j][:, :, :].rearrange("p r n -> p (r n)")

            def proj(i, k, m0, m1):
                if m0 == 0:
                    pe.wait_ge(s_xt[k % 2], turn(i, k, 16, 16))
                    if from_chunk(i, k, 3):
                        pe.wait_ge(s_vw, num(i, k, 1, -2))
                    if from_chunk(i, k, 1):
                        pe.wait_ge(s_xrb, num(i, k))
                for m in range(m0, m1):
                    for kt in range(KT):
                        pe.matmul(pa[:, 128 * m:128 * m + 128], win[:, kt, 128 * m:128 * m + 128],
                                  xt[k % 2][:, kt, :].rearrange("p (q r b) -> p r q b", q=4, r=4),
                                  start=(kt == 0), stop=False)
                    mm = pe.matmul(pa[:, 128 * m:128 * m + 128], cond[:, 128 * m:128 * m + 128], ind8[:, :],
                                   start=False, stop=True)
                if m1 == MT:
                    mm.then_inc(s_xr, 1)

            def turn_conv(i, k):
                pe.wait_ge(s_xc, num(i, k, 1, 1))
                if from_chunk(i, k, 2):
                    pe.wait_ge(s_xnts, num(i, k, 1, -1))
                if from_chunk(i, k, 4):
                    pe.wait_ge(s_yts, num(i, k, 1, -3))
                for m in range(MT):
                    mm = pe.transpose(pb[:, 128 * m:128 * m + 128], xc[k % 2][:, m, :], ident[:, :])
                mm.then_inc(s_xct, 1)

            def turn_xn(i, k, hist=True):
                pe.wait_ge(s_xn, num(i, k, 1, 1))
                pe.wait_ge(s_xhat, num(i, k, 1, 1))
                if from_chunk(i, k, 3):
                    pe.wait_ge(s_yts, num(i, k, 1, -2))
                for m in range(MT):
                    mm = pe.transpose(pb[:, 128 * m:128 * m + 128], xn[k % 2][:, 128 * m:128 * m + 128], ident[:, :])
                mm.then_inc(s_xnt, 1)

            def token_coef(i, k):
                pe.wait_ge(s_xnts, num(i, k, 1, 1))
                if from_chunk(i, k, 3):
                    pe.wait_ge(s_fin, num(i, k, 1, -2))
                for m in range(MT):
                    mm = pe.matmul(pg[:, Z], xnT[:, m, :], wx[:, m, :], start=(m == 0), stop=(m == MT - 1))
                mm.then_inc(s_z, 1)

            def row_coef(i, k):
                pe.wait_ge(s_zx, num(i, k, 3, 3))
                for n in range(3):
                    mm = pe.matmul(pg[:, BLK + T * n:BLK + T * n + T], zx[:, n, :, :].rearrange("p b s -> p (b s)"),
                                   tsel[:, :], start=True, stop=True)
                mm.then_inc(s_blk, 1)

            def turn_spread(i, k):
                pe.wait_ge(s_sp, num(i, k, 1, 1))
                pe.wait_ge(s_xrb, stage(i, k, 3))
                for n in range(T // 2):
                    mm = pe.transpose(pab[:, 128 * n:128 * n + 128],
                                      spread[:, 2 * n:2 * n + 2, :].rearrange("p t j -> p (t j)"), identb[:, :])
                mm.then_inc(s_vt, 1)

            def gate(i, k, kt):
                if kt == 0:
                    pe.wait_ge(s_bk[k % 2], turn(i, k, 48, 48))
                    if from_chunk(i, k, 2):
                        pe.wait_ge(s_fin, num(i, k, 1, -1))
                    pe.wait_ge(s_th, stage(i, k, 2))
                    pe.wait_ge(s_bc, stage(i, k, 2))
                mm = pe.matmul(pg[:, :], xtb[k % 2][:, kt, :], win[:, kt, DI:2 * DI], start=(kt == 0), stop=(kt == KT - 1))
                if kt == KT - 1:
                    mm.then_inc(s_gate, 1)

            def turn_y(i, k):
                pe.wait_ge(s_ygs, num(i, k, 1, 1))
                pe.wait_ge(s_xhat, stage(i, k, 4))
                for m in range(MT):
                    mm = pe.transpose(pb[:, 128 * m:128 * m + 128], yg[:, 128 * m:128 * m + 128], ident[:, :])
                mm.then_inc(s_yt, 1)

            def project_out(i, k, m0, m1):
                if m0 == 0:
                    pe.wait_ge(s_yts, num(i, k, 1, 1))
                    pe.wait_ge(s_sg, stage(i, k, 2))
                    if from_chunk(i, k, 1):
                        pe.wait_ge(s_fin, num(i, k))
                for m in range(m0, m1):
                    mm = pe.matmul(pg[:, OUT], ygT[:, m, :], wout[:, m, :], start=(m == 0), stop=(m == MT - 1))
                if m1 == MT:
                    mm.then_inc(s_o, 1)

            def pair(i, fixed=None):
                for k in range(2):
                    c = 4 if fixed is None else 2 * fixed + k
                    for s in range(T):
                        if s + AHEAD < T:
                            step_product(i, k, s + AHEAD)
                        elif c + 1 < NCH:
                            step_product(i, k + 1, s + AHEAD - T)
                        if s == 0 and c >= 2:
                            project_out(i, k - 2, 2, 4)
                        if s == 0 and c + 1 < NCH:
                            turn_xn(i, k + 1)
                        if s == 1 and c >= 1:
                            y_group(i, k - 1, 3)
                        if s == 3 and c + 1 < NCH:
                            token_coef(i, k + 1)
                        if s in (2, 3, 6, 7) and c + 3 < NCH:
                            m = (2, 3, 6, 7).index(s)
                            proj(i, k + 3, m, m + 1)
                        if s in (5, 9, 13):
                            y_group(i, k, s // 4 - 1)
                        if s == 5 and c + 2 < NCH:
                            turn_conv(i, k + 2)
                        if s == 6 and c + 1 < NCH:
                            row_coef(i, k + 1)
                        if s == 10 and c + 1 < NCH:
                            turn_spread(i, k + 1)
                        if s in (11, 12):
                            gate(i, k, s - 11)
                        if s == 13 and c >= 1:
                            turn_y(i, k - 1)
                        if s == 15 and c >= 1:
                            project_out(i, k - 1, 0, 2)

            pe.wait_ge(s_const, CONST)
            for m in range(MT):
                mm = pe.matmul(pg[:, NS * m:NS * m + NS], wxdt[:, 128 * m:128 * m + 128], wdt[:, :], start=True, stop=True)
            mm.then_inc(s_wdt, 1)
            pe.wait_ge(s_wx, 1)
            pe.wait_ge(s_idb, 1)
            proj(0, 0, 0, 4)
            proj(0, 1, 0, 4)
            turn_conv(0, 0)
            turn_xn(0, 0)
            token_coef(0, 0)
            row_coef(0, 0)
            turn_conv(0, 1)
            pe.wait_ge(s_sp, 1)
            pe.wait_ge(s_xrb, 2)
            for n in range(T // 2):
                mm = pe.transpose(pab[:, 128 * n:128 * n + 128],
                                  spread[:, 2 * n:2 * n + 2, :].rearrange("p t j -> p (t j)"), identb[:, :])
            mm.then_inc(s_vt, 1)
            pe.wait_ge(s_vw, 1)
            proj(0, 2, 0, 4)
            for s in range(AHEAD):
                step_product(0, 0, s)
            pair(0, 0)
            pair(1, 1)
            with pe.Fori(MAIN.start, MAIN.stop) as i:
                pair(i)
            pair(14, 14)
            pair(15, 15)
            project_out(15, 0, 2, 4)
            y_group(15, 1, 3)
            turn_y(15, 1)
            project_out(15, 1, 0, 4)

        @block.vector
        def _(dve):
            def scan_pre(i, k, s):
                if s == 0:
                    dve.wait_ge(s_ad, num(i, k, 1, 1))
                dve.wait_ge(s_v, num(i, k, T, s + 1))
                if s >= 1 or from_chunk(i, k, 1):
                    dve.wait_ge(s_h, num(i, k, T, s))
                dve.scalar_tensor_tensor(out=pre[:, :], in0=h[:, (s - 1) % 8, :], scalar=ad[k % 2][:, place(s):place(s) + 1],
                                         in1=pv[s % 4][:, :], op0=ALU.mult, op1=ALU.add).then_inc(s_pre, 1)

            def scan_clip(i, k, s):
                dve.wait_ge(s_pre, num(i, k, T, s + 1))
                if s % 4 == 0 and (s >= 8 or from_chunk(i, k, 1)):
                    dve.wait_ge(s_yg, num(i, k, T // 4, s // 4 - 1))
                dve.tensor_scalar(h[:, s % 8, :], pre[:, :], -CLIP, CLIP, ALU.max, ALU.min).then_inc(s_h, 1)

            def norm_stats(i, k):
                dve.wait_ge(s_xct, num(i, k, 1, 1))
                if from_chunk(i, k, 1):
                    dve.wait_ge(s_nmr, num(i, k))
                dve.bn_stats(stats[:, :], pb[:, :]).then_inc(s_st, 1)

            def norm_mean(i, k):
                made, = ready_values(dve, num(i, k, 2, 1))
                dve.wait_ge(*READY)
                dve.wait_ge(s_st, made)
                dve.bn_aggr(mv[:, :], stats[:, :]).then_inc(s_st, 1)

            def norm_cap(i, k):
                dve.wait_ge(s_ss, num(i, k, 1, 1))
                dve.tensor_scalar(sscap[:, :], ss[k % 2][:, :], 1.0, None, ALU.min).then_inc(s_cap, 1)

            def scale_b(i, k):
                dve.wait_ge(s_z, num(i, k, 1, 1))
                dve.wait_ge(s_ncap, num(i, k, 1, 1))
                dve.tensor_scalar(zs[:, 0:NS], pg[:, 0:NS], ncap[:, 0:1], None, ALU.mult).then_inc(s_zb, 1)

            def copy_rows(i, k):
                dve.wait_ge(s_th, num(i, k, 1, 1))
                if from_chunk(i, k, 1):
                    dve.wait_ge(s_sp, num(i, k))
                if from_chunk(i, k, 1):
                    dve.wait_ge(s_cw, num(i, k))
                dve.tensor_copy(bc[:, :, :].rearrange("p n t -> p (n t)"), pg[:, BLK:BLK + 2 * T]).then_inc(s_bc, 1)

            def add_skip(i, k):
                dve.wait_ge(s_yg, num(i, k, 4, 4))
                dve.wait_ge(s_dxn, num(i, k, 1, 1))
                if from_chunk(i, k, 1):
                    dve.wait_ge(s_ygs, num(i, k))
                dve.tensor_tensor(y1[:, :], py[:, :], dxn[:, :], ALU.add).then_inc(s_y1, 1)

            def residual(i, k):
                dve.wait_ge(s_o, num(i, k, 1, 1))
                if from_chunk(i, k, 2):
                    dve.wait_ge(s_out[k % 2], turn(i, k, 16))
                dve.tensor_tensor(fin[k % 2][:, :], pg[:, OUT], xres[k % 2][:, :], ALU.add).then_inc(s_fin, 1)

            def pair(i, fixed=None):
                for k in range(2):
                    c = 4 if fixed is None else 2 * fixed + k
                    for s in range(T):
                        scan_pre(i, k, s)
                        scan_clip(i, k, s)
                        if s == 0 and c + 1 < NCH:
                            norm_cap(i, k + 1)
                        if s == 2 and c >= 2:
                            residual(i, k - 2)
                        if s == 3 and c >= 1:
                            add_skip(i, k - 1)
                        if s == 4 and c + 1 < NCH:
                            scale_b(i, k + 1)
                        if s == 6 and c + 2 < NCH:
                            norm_stats(i, k + 2)
                        if s == 7 and c + 2 < NCH:
                            norm_mean(i, k + 2)
                        if s == 8 and c + 1 < NCH:
                            copy_rows(i, k + 1)

            dve.memset(xrb[0][:, :, 0:HIST], 0.0).then_inc(s_zero, 1)
            dve.memset(h[:, 7, :], 0.0).then_inc(s_zero, 1)
            dve.memset(spread[:, :, :], 0.0).then_inc(s_zero, 1)
            for j in range(2):
                dve.memset(cw[j][:, :, :], 0.0).then_inc(s_zero, 1)
            dve.wait_ge(s_const, CONST)
            dve.tensor_copy(identb[:, :], ident[:, :]).then_inc(s_idb, 1)
            dve.wait_ge(s_wdt, 1)
            dve.tensor_copy(wx[:, :, 2 * NS:], pg[:, 0:NS * MT].rearrange("p (m n) -> p m n", m=MT)).then_inc(s_wx, 1)
            for f, k in ((norm_stats, 0), (norm_mean, 0), (norm_cap, 0), (scale_b, 0),
                         (copy_rows, 0), (norm_stats, 1), (norm_mean, 1)):
                f(0, k)
            dve.wait_ge(s_zero, 5)
            pair(0, 0)
            pair(1, 1)
            with dve.Fori(MAIN.start, MAIN.stop) as i:
                pair(i)
            pair(14, 14)
            pair(15, 15)
            residual(15, 0)
            add_skip(15, 1)
            residual(15, 1)

        @block.scalar
        def _(act):
            def proj_out(i, k):
                act.wait_ge(s_xr, num(i, k, 1, 1))
                product = pa[:, :].rearrange("p (m n) -> p m n", m=MT)
                act.activation(xrb[k % 2][:, :, HIST:], product, ACT.Copy)
                act.activation(xrb[(k + 1) % 2][:, :, 0:HIST], product[:, :, 128 - HIST:], ACT.Copy).then_inc(s_xrb, 1)

            def conv_taps(i, k, first, last):
                if first == 0:
                    act.wait_ge(s_xrb, num(i, k, 1, 1))
                    if from_chunk(i, k, 1):
                        act.wait_ge(s_cv, num(i, k, 3))
                for n in range(first, last):
                    for m in range(MT):
                        a = act.activation(tap[n][:, m, :], xrb[k % 2][:, m, NB * n:NB * n + 128], ACT.Copy,
                                           scale=wconv[:, m, n:n + 1])
                if last == TAPS:
                    a.then_inc(s_tap, 1)

            def conv_silu(i, k):
                act.wait_ge(s_cv, num(i, k, 3, 3))
                if from_chunk(i, k, 2):
                    act.wait_ge(s_xct, num(i, k, 1, -1))
                for m in range(MT):
                    a = act.activation(xc[k % 2][:, m, :].rearrange("p (q r b) -> p q r b", q=4, r=4),
                                       conv[:, m, :].rearrange("p (r q b) -> p q r b", q=4, r=4), ACT.Silu,
                                       bias=bconv[:, m:m + 1])
                a.then_inc(s_xc, 1)

            def normalise(i, k):
                act.wait_ge(s_nmr, num(i, k, 1, 1))
                if from_chunk(i, k, 1):
                    act.wait_ge(s_xg, num(i, k))
                act.activation(xhat[:, :], pb[:, :], ACT.Identity, bias=nmr[:, 0:1], scale=rstd[:, 0:1]
                               ).then_inc(s_xhat, 1)

            def part_1(i, k):
                act.wait_ge(s_xn, num(i, k, 1, 1))
                if from_chunk(i, k, 2):
                    act.wait_ge(s_scr[k % 2], turn(i, k, 64))
                act.activation(xp[0][k % 2][:, :], xn[k % 2][:, :], ACT.Copy).then_inc(s_x1, 1)

            def square(i, k):
                if from_chunk(i, k, 2):
                    act.wait_ge(s_cap, num(i, k, 1, -1))
                act.activation(sq[:, :], xn[k % 2][:, :], ACT.Square, accum_out=ss[k % 2][:, :]).then_inc(s_ss, 1)

            def part_2(i, k):
                act.wait_ge(s_r1, num(i, k, 1, 1))
                act.activation(xp[1][k % 2][:, :], res[:, :], ACT.Copy).then_inc(s_x2, 1)

            def xn_by_channel(i, k):
                act.wait_ge(s_xnt, num(i, k, 1, 1))
                if from_chunk(i, k, 1):
                    act.wait_ge(s_z, num(i, k))
                act.activation(xnT[:, :, :].rearrange("p m n -> p (m n)"), pb[:, :], ACT.Copy).then_inc(s_xnts, 1)

            def copy_c_dt(i, k):
                act.wait_ge(s_zb, num(i, k, 1, 1))
                if from_chunk(i, k, 1):
                    act.wait_ge(s_zx, num(i, k, 3))
                act.activation(zs[:, NS:], pg[:, NS:3 * NS], ACT.Copy).then_inc(s_zc, 1)

            def tanh_dt(i, k):
                act.wait_ge(s_blk, num(i, k, 1, 1))
                if from_chunk(i, k, 1):
                    act.wait_ge(s_ad, num(i, k))
                act.activation(th[:, :], pg[:, BLK + 2 * T:BLK + 3 * T], ACT.Tanh, bias=bdt[:, 0:1]).then_inc(s_th, 1)

            def bd_parts_out(i, k):
                act.wait_ge(s_vt, num(i, k, 1, 1))
                if from_chunk(i, k, 2):
                    act.wait_ge(s_v, num(i, k, T, -T))
                act.activation(vw[k % 2][:, :, :].rearrange("p n m -> p (n m)"), pab[:, :], ACT.Copy).then_inc(s_vw, 1)

            def gate_silu(i, k):
                act.wait_ge(s_gate, num(i, k, 1, 1))
                if from_chunk(i, k, 1):
                    act.wait_ge(s_ygs, num(i, k))
                act.activation(sg[:, :], pg[:, :], ACT.Silu).then_inc(s_sg, 1)

            def y_by_channel(i, k):
                act.wait_ge(s_yt, num(i, k, 1, 1))
                if from_chunk(i, k, 1):
                    act.wait_ge(s_o, num(i, k))
                act.activation(ygT[:, :, :].rearrange("p m n -> p (m n)"), pb[:, :], ACT.Copy).then_inc(s_yts, 1)

            def pair(i, fixed=None):
                for k in range(2):
                    c = 4 if fixed is None else 2 * fixed + k
                    if c + 1 < NCH:
                        xn_by_channel(i, k + 1)
                    if c + 2 < NCH:
                        conv_silu(i, k + 2)
                    if c + 1 < NCH:
                        copy_c_dt(i, k + 1)
                        tanh_dt(i, k + 1)
                    if c + 3 < NCH:
                        proj_out(i, k + 3)
                        conv_taps(i, k + 3, 0, 1)
                    if c + 2 < NCH:
                        normalise(i, k + 2)
                    if c + 3 < NCH:
                        conv_taps(i, k + 3, 1, 2)
                    if c + 1 < NCH:
                        bd_parts_out(i, k + 1)
                    if c + 3 < NCH:
                        conv_taps(i, k + 3, 2, 3)
                    if c + 2 < NCH:
                        part_1(i, k + 2)
                        square(i, k + 2)
                    gate_silu(i, k)
                    if c + 3 < NCH:
                        conv_taps(i, k + 3, 3, TAPS)
                    if c + 2 < NCH:
                        part_2(i, k + 2)
                    if c >= 1:
                        y_by_channel(i, k - 1)

            act.wait_ge(s_const, CONST)
            act.activation(acol[:, :], alog[:, :], ACT.Tanh).then_inc(s_acol, 1)
            act.wait_ge(s_zero, 1)
            proj_out(0, 0)
            conv_taps(0, 0, 0, TAPS)
            conv_silu(0, 0)
            proj_out(0, 1)
            normalise(0, 0)
            part_1(0, 0)
            square(0, 0)
            part_2(0, 0)
            xn_by_channel(0, 0)
            copy_c_dt(0, 0)
            tanh_dt(0, 0)
            conv_taps(0, 1, 0, TAPS)
            conv_silu(0, 1)
            normalise(0, 1)
            bd_parts_out(0, 0)
            part_1(0, 1)
            square(0, 1)
            part_2(0, 1)
            proj_out(0, 2)
            conv_taps(0, 2, 0, TAPS)
            pair(0, 0)
            pair(1, 1)
            with act.Fori(MAIN.start, MAIN.stop) as i:
                pair(i)
            pair(14, 14)
            pair(15, 15)
            y_by_channel(15, 1)

        @block.gpsimd
        def _(pool):
            def conv_sum(i, k):
                pool.wait_ge(s_tap, num(i, k, 1, 1))
                if from_chunk(i, k, 1):
                    pool.wait_ge(s_xc, num(i, k))
                pool.tensor_tensor(conv[:, :, :], tap[0][:, :, :], tap[1][:, :, :], ALU.add).then_inc(s_cv, 1)
                for n in range(2, TAPS):
                    pool.wait_ge(s_cv, num(i, k, 3, n - 1))
                    pool.tensor_tensor(conv[:, :, :], conv[:, :, :], tap[n][:, :, :], ALU.add).then_inc(s_cv, 1)

            def norm_root(i, k):
                made, = ready_values(pool, num(i, k, 2, 2))
                pool.wait_ge(*READY)
                pool.wait_ge(s_st, made)
                pool.tensor_scalar(vare[:, :], mv[:, 1:2], 1e-5, None, ALU.add).then_inc(s_vare, 1)
                if from_chunk(i, k, 1):
                    pool.wait_ge(s_xhat, num(i, k))
                pool.wait_ge(s_vare, num(i, k, 1, 1))
                pool.tensor_tensor(rstd[:, :], vare[:, :], expo[:, 0:1], ALU.pow).then_inc(s_rstd, 1)
                made, = ready_values(pool, num(i, k, 1, 1))
                pool.wait_ge(*READY)
                pool.wait_ge(s_rstd, made)
                pool.tensor_scalar(nmr[:, :], mv[:, 0:1], rstd[:, 0:1], -1.0, ALU.mult, ALU.mult).then_inc(s_nmr, 1)

            def affine(i, k):
                pool.wait_ge(s_xhat, num(i, k, 1, 1))
                if from_chunk(i, k, 2):
                    pool.wait_ge(s_scr[k % 2], turn(i, k, 64))
                pool.tensor_tensor(xg[:, :], xhat[:, :], gain[:, :], ALU.mult).then_inc(s_xg, 1)
                pool.wait_ge(s_xg, num(i, k, 1, 1))
                pool.tensor_tensor(xn[k % 2][:, :], xg[:, :], beta[:, :], ALU.add).then_inc(s_xn, 1)

            def residue_1(i, k):
                pool.wait_ge(s_x1, num(i, k, 1, 1))
                if from_chunk(i, k, 1):
                    pool.wait_ge(s_x3, num(i, k))
                pool.tensor_tensor(res[:, :], xn[k % 2][:, :], xp[0][k % 2][:, :], ALU.subtract).then_inc(s_r1, 1)

            def part_3(i, k):
                pool.wait_ge(s_x2, num(i, k, 1, 1))
                if from_chunk(i, k, 2):
                    pool.wait_ge(s_scr[k % 2], turn(i, k, 64))
                pool.tensor_tensor(xp[2][k % 2][:, :], res[:, :], xp[1][k % 2][:, :], ALU.subtract).then_inc(s_x3, 1)

            def cap_root(i, k):
                pool.wait_ge(s_cap, num(i, k, 1, 1))
                if from_chunk(i, k, 1):
                    pool.wait_ge(s_zb, num(i, k))
                pool.tensor_tensor(ncap[:, :], sscap[:, :], expo[:, 1:2], ALU.pow).then_inc(s_ncap, 1)

            def spread_tokens(i, k):
                pool.wait_ge(s_zb, num(i, k, 1, 1))
                pool.wait_ge(s_zc, num(i, k, 1, 1))
                if from_chunk(i, k, 1):
                    pool.wait_ge(s_blk, num(i, k))
                for n in range(3):
                    pool.tensor_tensor(zx[:, n, :, :], bcast(zs[:, NS * n:NS * n + NS], 1, NB),
                                       bcast(tokmask[:, :], 2, NS), ALU.mult).then_inc(s_zx, 1)

            def decay(i, k):
                made, read = ready_values(pool, num(i, k, 1, 1), num(i, k, T, -T))
                pool.wait_ge(*READY)
                pool.wait_ge(s_th, made)
                if from_chunk(i, k, 2):
                    pool.wait_ge(s_pre, read)
                pool.tensor_scalar(ad[k % 2][:, :], th[:, :], acol[:, 0:1], 1.0, ALU.mult, ALU.add).then_inc(s_ad, 1)

            def bd_parts(i, k):
                made, = ready_values(pool, num(i, k, 1, 1))
                pool.wait_ge(*READY)
                pool.wait_ge(s_bc, made)
                pool.tensor_copy(bp[0][:, :], bc[:, 0, :]).then_inc(s_bp, 1)
                pool.wait_ge(s_bp, num(i, k, 4, 1))
                pool.tensor_tensor(bres[:, :], bc[:, 0, :], bp[0][:, :], ALU.subtract).then_inc(s_bp, 1)
                made, = ready_values(pool, num(i, k, 4, 2))
                pool.wait_ge(*READY)
                pool.wait_ge(s_bp, made)
                pool.tensor_copy(bp[1][:, :], bres[:, :]).then_inc(s_bp, 1)
                pool.wait_ge(s_bp, num(i, k, 4, 3))
                pool.tensor_tensor(bp[2][:, :], bres[:, :], bp[1][:, :], ALU.subtract).then_inc(s_bp, 1)

            def spread_rows(i, k):
                pool.wait_ge(s_bp, num(i, k, 4, 4))
                if from_chunk(i, k, 1):
                    pool.wait_ge(s_vt, num(i, k))
                for n, p in enumerate(BPART):
                    last = pool.tensor_tensor(spread[:, :, NB * n:NB * n + NB], bcast(bp[p][:, :], 2, NB),
                                              bcast(rowmask[:, :], 1, T), ALU.mult)
                last.then_inc(s_sp, 1)
                if from_chunk(i, k, 2):
                    pool.wait_ge(s_yg, num(i, k, 4, -4))
                for odd in range(2):
                    last = pool.tensor_tensor(
                        cw[k % 2][:, :, 0:128].rearrange("p r (q n) -> p r q n", q=2)[:, :, :, 32 * odd:32 * odd + NB],
                        bcast(bc[:, 1, 8 * odd:8 * odd + 8].rearrange("p (r q) -> p r q", r=4), 3, NB),
                        bcast(bcast(rowmask[:, :], 1, 2), 1, 4), ALU.mult)
                last.then_inc(s_cw, 1)

            def skip(i, k):
                pool.wait_ge(s_bk[k % 2], turn(i, k, 48, 48))
                if from_chunk(i, k, 1):
                    pool.wait_ge(s_y1, num(i, k))
                pool.tensor_tensor(dxn[:, :], xnb[k % 2][:, :], dskip[:, :], ALU.mult).then_inc(s_dxn, 1)

            def gated(i, k):
                pool.wait_ge(s_sg, num(i, k, 1, 1))
                pool.wait_ge(s_y1, num(i, k, 1, 1))
                if from_chunk(i, k, 1):
                    pool.wait_ge(s_yt, num(i, k))
                pool.tensor_tensor(yg[:, :], y1[:, :], sg[:, :], ALU.mult).then_inc(s_ygs, 1)

            def pair(i, fixed=None):
                for k in range(2):
                    c = 4 if fixed is None else 2 * fixed + k
                    if c + 1 < NCH:
                        cap_root(i, k + 1)
                    if c + 2 < NCH:
                        conv_sum(i, k + 2)
                    if c >= 1:
                        gated(i, k - 1)
                    if c + 1 < NCH:
                        spread_tokens(i, k + 1)
                    if c + 2 < NCH:
                        norm_root(i, k + 2)
                    if c + 1 < NCH:
                        decay(i, k + 1)
                        bd_parts(i, k + 1)
                        spread_rows(i, k + 1)
                    if c + 2 < NCH:
                        affine(i, k + 2)
                    if c + 2 < NCH:
                        residue_1(i, k + 2)
                    skip(i, k)
                    if c + 2 < NCH:
                        part_3(i, k + 2)

            pool.wait_ge(s_const, CONST)
            pool.wait_ge(s_acol, 1)
            pool.tensor_scalar(acol[:, :], acol[:, :], -0.01, None, ALU.mult).then_inc(s_acol, 1)
            pool.wait_ge(s_zero, 5)
            pool.wait_ge(s_acol, 2)
            conv_sum(0, 0)
            norm_root(0, 0)
            affine(0, 0)
            residue_1(0, 0)
            part_3(0, 0)
            cap_root(0, 0)
            spread_tokens(0, 0)
            conv_sum(0, 1)
            decay(0, 0)
            bd_parts(0, 0)
            spread_rows(0, 0)
            norm_root(0, 1)
            affine(0, 1)
            residue_1(0, 1)
            part_3(0, 1)
            pair(0, 0)
            pair(1, 1)
            with pool.Fori(MAIN.start, MAIN.stop) as i:
                pair(i)
            pair(14, 14)
            pair(15, 15)
            gated(15, 1)


def host_layout(a):
    def turned(w, tiles):
        return np.ascontiguousarray(w.T.reshape(tiles, 128, w.shape[0]).transpose(1, 0, 2))

    def per_channel(w):
        return np.ascontiguousarray(w.reshape(MT, 128, -1).transpose(1, 0, 2))

    def on_all(v):
        return np.ascontiguousarray(np.broadcast_to(v[None, :], (128, v.shape[0])))

    def on_rows(v):
        return np.ascontiguousarray(np.broadcast_to(v[None, :], (NB, NS)).reshape(128, 1))

    x = np.ascontiguousarray(a["x"].reshape(NB, NCH, 4, 4, DM).transpose(1, 3, 2, 0, 4).reshape(NCH, 128, DM))
    xT = np.ascontiguousarray(x.reshape(NCH, 128, KT, 128).transpose(0, 3, 2, 1))
    p = np.arange(128)
    column = 2 * (p // 8 % 8) + p // 64
    f = np.float32
    pre = "L0_cond_"
    return {
        "x": x, "xT": xT, "w_in": turned(a[pre + "W_in"], KT), "w_out": turned(a[pre + "W_out"], MT),
        "w_xp": turned(a[pre + "W_xproj"], MT), "w_xdt": np.ascontiguousarray(a[pre + "W_xproj"][2 * NS:]),
        "w_dt": np.ascontiguousarray(a[pre + "W_dt"].T), "cond": np.ascontiguousarray(a["cond_2048"]),
        "ind8": (p[None, :] % NB == np.arange(NB)[:, None]).astype(f),
        "w_conv": per_channel(a[pre + "W_conv"]), "b_conv": per_channel(a[pre + "b_conv"])[:, :, 0].copy(),
        "gain": on_all(a[pre + "ln_g"]), "beta": on_all(a[pre + "ln_b"]), "dskip": on_all(a[pre + "D"]),
        "alog": on_rows(a[pre + "A_log"]), "b_dt": on_rows(a[pre + "b_dt"]), "ident": np.eye(128, dtype=f),
        "rowmask": (p[:, None] // NS == np.arange(NB)[None, :]).astype(f),
        "tokmask": (p[:, None] % NB == np.arange(NB)[None, :]).astype(f),
        "tsel": (column[:, None] == np.arange(T)[None, :]).astype(f),
        "expo": np.ascontiguousarray(np.broadcast_to(np.array([-0.5, 0.5], f), (128, 2))),
    }


def declare(nc, arrays):
    d = {n: nc.dram_tensor(f"in_{n}", v.shape, F32, kind="ExternalInput").ap() for n, v in arrays.items()}
    d["out"] = nc.dram_tensor("out_0", (NCH, 128, DM), F32, kind="ExternalOutput").ap()
    return d


def kernel(**inputs):
    import concourse.bacc as _bacc
    from concourse.bass_utils import run_bass_kernel_spmd as run

    arrays = host_layout({k: np.asarray(v) for k, v in inputs.items()})
    nc = _bacc.Bacc("TRN2", target_bir_lowering=False, num_devices=1)
    build(nc, declare(nc, arrays))
    r = run(nc, [{f"in_{n}": v for n, v in arrays.items()}], core_ids=[0])
    out = r.results[0]["out_0"].reshape(NCH, 4, 4, NB, DM)
    return np.ascontiguousarray(out.transpose(3, 0, 2, 1, 4).reshape(NB, SEQ, DM))
```

```python
from contextlib import ExitStack

import numpy as np

import concourse.bass as bass
from concourse import mybir

F32 = mybir.dt.float32
BF16 = mybir.dt.bfloat16
ALU = mybir.AluOpType
ACT = mybir.ActivationFunctionType

NB, SEQ, DM = 8, 512, 256
DI, NS = 512, 16
T = 16
NCH = SEQ // T
TAPS = 4
MT, KT = DI // 128, DM // 128
HIST = (TAPS - 1) * NB
CLIP = 10.0
XPART = (0, 0, 0, 1, 1, 2)
BPART = (0, 1, 2, 0, 1, 0)
NJ = len(XPART)
KV = NJ * NB
AHEAD = 3
MAIN = range(2, 14)


def from_chunk(i, k, first):
    return not isinstance(i, int) or 2 * i + k >= first


def ready_values(eng, *values):
    for value in values:
        if not isinstance(value, int):
            eng.compute_val(value)
    return values


def place(s):
    q, r = s % 4, s // 4
    return 8 * (q % 2) + 2 * r + q // 2


def bcast(ap, axis, n):
    ap = ap.unsqueeze(axis)
    shape = list(ap.shape)
    shape[axis] = n
    return ap.to_broadcast(shape)


def build(nc, d):
    with ExitStack() as ctx:
        def sb(name, shape, dt=F32):
            return ctx.enter_context(nc.sbuf_tensor(name, shape, dt))

        def psum(name):
            return ctx.enter_context(nc.psum_tensor(name, [128, 512], F32))

        def sem(name):
            return ctx.enter_context(nc.semaphore(name))

        xp_dram = nc.dram_tensor("xp_scratch", (3, NCH, 128, DI), BF16, kind="Internal").ap()

        win = sb("win", [128, KT, 2 * DI])
        wout = sb("wout", [128, MT, DM])
        wx = sb("wx", [128, MT, 3 * NS])
        wxdt = sb("wxdt", [NS, DI])
        wdt = sb("wdt", [NS, NS])
        cond = sb("cond", [NB, DI])
        ind8 = sb("ind8", [NB, 128])
        wconv = sb("wconv", [128, MT, TAPS])
        bconv = sb("bconv", [128, MT])
        gain = sb("gain", [128, DI])
        beta = sb("beta", [128, DI])
        dcol = sb("dcol", [128, MT])
        ddiag = sb("ddiag", [128, MT, 128])
        alog = sb("alog", [128, 1])
        acol = sb("acol", [128, 1])
        bdt = sb("bdt", [128, 1])
        ident = sb("ident", [128, 128])
        identb = sb("identb", [128, 128], BF16)
        rowmask = sb("rowmask", [128, NB])
        tokmask = sb("tokmask", [128, NB])
        tsel = sb("tsel", [128, T])
        expo = sb("expo", [128, 2])

        xt = [sb(f"xt{j}", [128, KT, 128]) for j in range(2)]
        xrb = [sb(f"xrb{j}", [128, MT, HIST + 128]) for j in range(2)]
        conv = sb("conv", [128, MT, 128])
        tap = [sb(f"tap{n}", [128, MT, 128]) for n in range(TAPS)]
        xc = [sb(f"xc{j}", [128, MT, 128]) for j in range(2)]
        stats = sb("stats", [128, 4, 6])
        mv = sb("mv", [128, 2])
        vare = sb("vare", [128, 1])
        rstd = sb("rstd", [128, 1])
        nmr = sb("nmr", [128, 1])
        xhat = sb("xhat", [128, DI])
        xg = sb("xg", [128, DI])
        xn = [sb(f"xn{j}", [128, DI]) for j in range(2)]
        sq = sb("sq", [128, DI])
        ss = [sb(f"ss{j}", [128, 1]) for j in range(2)]
        res = sb("res", [128, DI])
        xp = [[sb(f"xp{p}_{j}", [128, DI], BF16) for j in range(2)] for p in range(3)]
        xnT = [sb(f"xnT{j}", [128, MT, 128]) for j in range(2)]
        sscap = sb("sscap", [128, 1])
        ncap = sb("ncap", [128, 1])
        zs = sb("zs", [128, 3 * NS])
        zx = sb("zx", [128, 3, NB, NS])
        th = sb("th", [128, T])
        bc = sb("bc", [128, 2, T])
        bres = sb("bres", [128, T])
        bp = [sb(f"bp{p}", [128, T], BF16) for p in range(3)]
        spread = sb("spread", [128, T, 64], BF16)
        ad = [sb(f"ad{j}", [128, T]) for j in range(2)]
        vw = [sb(f"vw{j}", [128, T // 2, 128], BF16) for j in range(2)]
        cw = [sb(f"cw{j}", [128, 4, 136]) for j in range(2)]
        xr = [sb(f"xr{j}", [128, T // 2, DI], BF16) for j in range(2)]
        pre = sb("pre", [128, DI])
        h = sb("h", [128, 8, DI])
        xtb = [sb(f"xtb{j}", [128, KT, 128]) for j in range(2)]
        xres = [sb(f"xres{j}", [128, DM]) for j in range(2)]
        sg = sb("sg", [128, DI])
        yg = sb("yg", [128, DI])
        ygT = sb("ygT", [128, MT, 128])
        fin = [sb(f"fin{j}", [128, DM]) for j in range(2)]

        pv = [psum(f"pv{j}") for j in range(4)]
        py = psum("py")
        pa = psum("pa")
        pb = psum("pb")
        pg = psum("pg")
        pab = pa[:, :].bitcast(BF16)
        Z, BLK, OUT = slice(0, 48), 64, slice(256, 512)

        s_first = sem("s_first")
        s_const = sem("s_const")
        s_later = sem("s_later")
        s_zero = sem("s_zero")
        s_wdt = sem("s_wdt")
        s_wx = sem("s_wx")
        s_acol = sem("s_acol")
        s_idb = sem("s_idb")
        s_xt = [sem(f"s_xt{j}") for j in range(2)]
        s_xr = sem("s_xr")
        s_xrb = sem("s_xrb")
        s_tap = sem("s_tap")
        s_cv = sem("s_cv")
        s_xc = sem("s_xc")
        s_xct = sem("s_xct")
        s_st = sem("s_st")
        s_vare = sem("s_vare")
        s_rstd = sem("s_rstd")
        s_nmr = sem("s_nmr")
        s_xhat = sem("s_xhat")
        s_xg = sem("s_xg")
        s_xn = sem("s_xn")
        s_ss = sem("s_ss")
        s_x1 = sem("s_x1")
        s_r1 = sem("s_r1")
        s_x2 = sem("s_x2")
        s_x3 = sem("s_x3")
        s_scr = [sem(f"s_scr{j}") for j in range(2)]
        s_xp = [sem(f"s_xp{j}") for j in range(2)]
        s_xnt = sem("s_xnt")
        s_xnts = sem("s_xnts")
        s_cap = sem("s_cap")
        s_ncap = sem("s_ncap")
        s_z = sem("s_z")
        s_zb = sem("s_zb")
        s_zc = sem("s_zc")
        s_zx = sem("s_zx")
        s_blk = sem("s_blk")
        s_th = sem("s_th")
        s_bc = sem("s_bc")
        s_ad = sem("s_ad")
        s_bp = sem("s_bp")
        s_sp = sem("s_sp")
        s_cw = sem("s_cw")
        s_vt = sem("s_vt")
        s_vw = sem("s_vw")
        s_v = sem("s_v")
        s_pre = sem("s_pre")
        s_h = sem("s_h")
        s_yg = sem("s_yg")
        s_bk = [sem(f"s_bk{j}") for j in range(2)]
        s_gate = sem("s_gate")
        s_sg = sem("s_sg")
        s_dd = sem("s_dd")
        s_dx = sem("s_dx")
        s_ygs = sem("s_ygs")
        s_yt = sem("s_yt")
        s_yts = sem("s_yts")
        s_o = sem("s_o")
        s_fin = sem("s_fin")
        s_out = [sem(f"s_out{j}") for j in range(2)]

        first = [(win[:, :, 0:DI], d["w_in"][:, :, 0:DI]), (cond[:, :], d["cond"]), (ind8[:, :], d["ind8"]),
                 (wconv[:, :, :], d["w_conv"])]
        consts = [(bconv[:, :], d["b_conv"]), (ident[:, :], d["ident"]), (expo[:, :], d["expo"]),
                  (gain[:, :], d["gain"]), (beta[:, :], d["beta"]), (wxdt[:, :], d["w_xdt"]), (wdt[:, :], d["w_dt"]),
                  (wx[:, :, :], d["w_xp"]), (tokmask[:, :], d["tokmask"]), (tsel[:, :], d["tsel"]),
                  (bdt[:, :], d["b_dt"]), (alog[:, :], d["alog"]), (rowmask[:, :], d["rowmask"]),
                  (dcol[:, :], d["dcol"])]
        later = [(win[:, :, DI:2 * DI], d["w_in"][:, :, DI:2 * DI]), (wout[:, :, :], d["w_out"])]
        FIRST, CONST, LATER = (16 * len(group) for group in (first, consts, later))
        READY = (s_first, FIRST)

        def num(i, k, per=1, more=0):
            return i * (2 * per) + (per * k + more)

        def turn(i, k, per=1, more=0):
            return i * per + (per * (k // 2) + more)

        def stage(i, k, ahead):
            return min(2 * i + k + ahead, NCH) if isinstance(i, int) else num(i, k, 1, ahead)

        block = ctx.enter_context(nc.Block())

        @block.sync
        def _(sp):
            def load_xt(i, k):
                if from_chunk(i, k, 2):
                    read, = ready_values(sp, num(i, k, 1, -1))
                    sp.wait_ge(*READY)
                    sp.wait_ge(s_xr, read)
                sp.dma_start(xt[k % 2][:, :, :], d["xT"][bass.ds(num(i, k), 1)].rearrange("o p k n -> (o p) k n")
                             ).then_inc(s_xt[k % 2], 16)

            def store_scratch(i, k):
                j = k % 2
                for p, ready in enumerate((s_x1, s_x2, s_x3)):
                    made, = ready_values(sp, num(i, k, 1, 1))
                    sp.wait_ge(*READY)
                    sp.wait_ge(ready, made)
                    sp.dma_start(xp_dram[p][bass.ds(num(i, k), 1)].rearrange("o p n -> (o p) n"), xp[p][j][:, :]
                                 ).then_inc(s_scr[j], 16)

            def load_xr(i, k):
                j = k % 2
                stored, read = ready_values(sp, turn(i, k, 48, 48), num(i, k, T, -T))
                sp.wait_ge(*READY)
                sp.wait_ge(s_scr[j], stored)
                if from_chunk(i, k, 2):
                    sp.wait_ge(s_v, read)
                for n, p in enumerate(XPART):
                    for e in range(2):
                        row = 64 * e + NB * n
                        sp.dma_start(xr[j][row:row + NB, :, :], xp_dram[p][bass.ds(num(i, k), 1), 64 * e:64 * e + 64]
                                     .rearrange("o (f b) n -> (o b) f n", b=NB)
                                     ).then_inc(s_xp[j], 16)

            def load_back(i, k):
                j = k % 2
                if from_chunk(i, k, 2):
                    read, = ready_values(sp, num(i, k, 1, -1))
                    sp.wait_ge(*READY)
                    sp.wait_ge(s_gate, read)
                    sp.wait_ge(s_fin, read)
                c = bass.ds(num(i, k), 1)
                sp.dma_start(xtb[j][:, :, :], d["xT"][c].rearrange("o p k n -> (o p) k n")).then_inc(s_bk[j], 16)
                sp.dma_start(xres[j][:, :], d["x"][c].rearrange("o p n -> (o p) n")).then_inc(s_bk[j], 16)

            def store_out(i, k):
                made, = ready_values(sp, num(i, k, 1, 1))
                sp.wait_ge(*READY)
                sp.wait_ge(s_fin, made)
                sp.dma_start(d["out"][bass.ds(num(i, k), 1)].rearrange("o p n -> (o p) n"), fin[k % 2][:, :]
                             ).then_inc(s_out[k % 2], 16)

            def pair(i, fixed=None):
                for k in range(2):
                    c = 4 if fixed is None else 2 * fixed + k
                    if c >= 2:
                        store_out(i, k - 2)
                    load_back(i, k)
                    if c + 1 < NCH:
                        load_xr(i, k + 1)
                    if c + 4 < NCH:
                        load_xt(i, k + 4)
                    if c + 2 < NCH:
                        store_scratch(i, k + 2)

            load_xt(0, 0)
            for dst, src in first:
                sp.dma_start(dst, src).then_inc(s_first, 16)
            for dst, src in consts:
                sp.dma_start(dst, src).then_inc(s_const, 16)
            load_xt(0, 1)
            for dst, src in later:
                sp.dma_start(dst, src).then_inc(s_later, 16)
            load_xt(0, 2)
            store_scratch(0, 0)
            load_xr(0, 0)
            load_xt(0, 3)
            store_scratch(0, 1)
            pair(0, 0)
            pair(1, 1)
            with sp.Fori(MAIN.start, MAIN.stop) as i:
                pair(i)
            pair(14, 14)
            pair(15, 15)
            store_out(15, 0)
            store_out(15, 1)
            for j in range(2):
                sp.wait_ge(s_out[j], 16 * NCH // 2)

        @block.tensor
        def _(pe):
            def step_product(i, k, s):
                j, slot, row = k % 2, place(s) // 2, 64 * (place(s) % 2)
                if s == 0:
                    pe.wait_ge(s_vw, num(i, k, 1, 1))
                    pe.wait_ge(s_xp[j], turn(i, k, 192, 192))
                if s >= 4 or from_chunk(i, k, 1):
                    pe.wait_ge(s_pre, num(i, k, T, s - 3))
                pe.matmul(pv[s % 4][:, :], vw[j][row:row + KV, slot, :], xr[j][row:row + KV, slot, :],
                          start=True, stop=True).then_inc(s_v, 1)

            def skip(i, k):
                if from_chunk(i, k, 1):
                    pe.wait_ge(s_ygs, num(i, k))
                for m in range(MT):
                    mm = pe.matmul(py[:, 128 * m:128 * m + 128], xnT[k % 2][:, m, :], ddiag[:, m, :],
                                   start=(m == 0), stop=False)
                mm.then_inc(s_dx, 1)

            def y_group(i, k, r):
                if r == 0:
                    pe.wait_ge(s_cw, num(i, k, 1, 1))
                pe.wait_ge(s_h, num(i, k, T, 4 * r + 4))
                for q in range(4):
                    mm = pe.matmul(py[32 * q:32 * q + 32, :], c_of(k % 2)[:, 128 * r + 32 * q:128 * r + 32 * q + 32],
                                   h[:, (4 * r + q) % 8, :], start=False, stop=(r == 3),
                                   tile_position=(0, 32 * q))
                mm.then_inc(s_yg, 1)

            def c_of(j):
                return cw[j][:, :, :].rearrange("p r n -> p (r n)")

            def proj(i, k, m0, m1, bank=pa):
                if m0 == 0:
                    pe.wait_ge(s_xt[k % 2], turn(i, k, 16, 16))
                    if from_chunk(i, k, 3):
                        pe.wait_ge(s_vw, num(i, k, 1, -2))
                    if from_chunk(i, k, 1):
                        pe.wait_ge(s_xrb, num(i, k))
                for m in range(m0, m1):
                    for kt in range(KT):
                        pe.matmul(bank[:, 128 * m:128 * m + 128], win[:, kt, 128 * m:128 * m + 128],
                                  xt[k % 2][:, kt, :].rearrange("p (q r b) -> p r q b", q=4, r=4),
                                  start=(kt == 0), stop=False)
                    mm = pe.matmul(bank[:, 128 * m:128 * m + 128], cond[:, 128 * m:128 * m + 128], ind8[:, :],
                                   start=False, stop=True)
                if m1 == MT:
                    mm.then_inc(s_xr, 1)

            def turn_conv(i, k):
                pe.wait_ge(s_xc, num(i, k, 1, 1))
                if from_chunk(i, k, 2):
                    pe.wait_ge(s_xnts, num(i, k, 1, -1))
                if from_chunk(i, k, 4):
                    pe.wait_ge(s_yts, num(i, k, 1, -3))
                for m in range(MT):
                    mm = pe.transpose(pb[:, 128 * m:128 * m + 128], xc[k % 2][:, m, :], ident[:, :])
                mm.then_inc(s_xct, 1)

            def turn_xn(i, k, hist=True):
                pe.wait_ge(s_xn, num(i, k, 1, 1))
                pe.wait_ge(s_xhat, num(i, k, 1, 1))
                if from_chunk(i, k, 3):
                    pe.wait_ge(s_yts, num(i, k, 1, -2))
                for m in range(MT):
                    mm = pe.transpose(pb[:, 128 * m:128 * m + 128], xn[k % 2][:, 128 * m:128 * m + 128], ident[:, :])
                mm.then_inc(s_xnt, 1)

            def token_coef(i, k):
                pe.wait_ge(s_xnts, num(i, k, 1, 1))
                if from_chunk(i, k, 3):
                    pe.wait_ge(s_fin, num(i, k, 1, -2))
                for m in range(MT):
                    mm = pe.matmul(pg[:, Z], xnT[k % 2][:, m, :], wx[:, m, :], start=(m == 0), stop=(m == MT - 1))
                mm.then_inc(s_z, 1)

            def row_coef(i, k):
                pe.wait_ge(s_zx, num(i, k, 3, 3))
                for n in range(3):
                    mm = pe.matmul(pg[:, BLK + T * n:BLK + T * n + T], zx[:, n, :, :].rearrange("p b s -> p (b s)"),
                                   tsel[:, :], start=True, stop=True)
                mm.then_inc(s_blk, 1)

            def turn_spread(i, k):
                pe.wait_ge(s_sp, num(i, k, 1, 1))
                pe.wait_ge(s_xrb, stage(i, k, 3))
                for n in range(T // 2):
                    mm = pe.transpose(pab[:, 128 * n:128 * n + 128],
                                      spread[:, 2 * n:2 * n + 2, :].rearrange("p t j -> p (t j)"), identb[:, :])
                mm.then_inc(s_vt, 1)

            def gate(i, k, n):
                half, kt = n // KT, n % KT
                cols = slice(256 * half, 256 * half + 256)
                if n == 0:
                    pe.wait_ge(s_bk[k % 2], turn(i, k, 32, 32))
                    if from_chunk(i, k, 2):
                        pe.wait_ge(s_fin, num(i, k, 1, -1))
                    pe.wait_ge(s_th, stage(i, k, 2))
                    pe.wait_ge(s_bc, stage(i, k, 2))
                mm = pe.matmul(pg[:, cols], xtb[k % 2][:, kt, :], win[:, kt, DI:][:, cols], start=(kt == 0), stop=(kt == KT - 1))
                if n == 3:
                    mm.then_inc(s_gate, 1)

            def turn_y(i, k):
                pe.wait_ge(s_ygs, num(i, k, 1, 1))
                pe.wait_ge(s_xhat, stage(i, k, 4))
                for m in range(MT):
                    mm = pe.transpose(pb[:, 128 * m:128 * m + 128], yg[:, 128 * m:128 * m + 128], ident[:, :])
                mm.then_inc(s_yt, 1)

            def project_out(i, k, m0, m1):
                if m0 == 0:
                    pe.wait_ge(s_yts, num(i, k, 1, 1))
                    pe.wait_ge(s_sg, stage(i, k, 2))
                    if from_chunk(i, k, 1):
                        pe.wait_ge(s_fin, num(i, k))
                for m in range(m0, m1):
                    mm = pe.matmul(pg[:, OUT], ygT[:, m, :], wout[:, m, :], start=(m == 0), stop=(m == MT - 1))
                if m1 == MT:
                    mm.then_inc(s_o, 1)

            def pair(i, fixed=None):
                for k in range(2):
                    c = 4 if fixed is None else 2 * fixed + k
                    for s in range(T):
                        if s + AHEAD < T:
                            step_product(i, k, s + AHEAD)
                        elif c + 1 < NCH:
                            step_product(i, k + 1, s + AHEAD - T)
                        if s == 0:
                            if c >= 1:
                                y_group(i, k - 1, 3)
                            if c + 3 < NCH:
                                proj(i, k + 3, 0, 1)
                        if s == 1:
                            if c + 1 < NCH:
                                turn_xn(i, k + 1)
                        if s == 2:
                            if c + 3 < NCH:
                                proj(i, k + 3, 1, 2)
                        if s == 3:
                            if c + 1 < NCH:
                                token_coef(i, k + 1)
                        if s == 4:
                            if c + 3 < NCH:
                                proj(i, k + 3, 2, 3)
                        if s == 5:
                            if c + 2 < NCH:
                                turn_conv(i, k + 2)
                            skip(i, k)
                            if c + 1 < NCH:
                                row_coef(i, k + 1)
                            y_group(i, k, 0)
                        if s == 7:
                            if c + 3 < NCH:
                                proj(i, k + 3, 3, 4)
                        if s == 8:
                            y_group(i, k, 1)
                        if s == 9:
                            if c + 1 < NCH:
                                turn_spread(i, k + 1)
                        if s == 10:
                            gate(i, k, 0)
                            gate(i, k, 1)
                        if s == 11:
                            gate(i, k, 2)
                        if s == 12:
                            gate(i, k, 3)
                        if s == 13:
                            y_group(i, k, 2)
                        if s == 14:
                            if c >= 1:
                                turn_y(i, k - 1)
                                project_out(i, k - 1, 0, 2)
                        if s == 15:
                            if c >= 1:
                                project_out(i, k - 1, 2, 4)

            pe.wait_ge(s_first, FIRST)
            proj(0, 0, 0, 4)
            pe.wait_ge(s_const, CONST)
            for m in range(MT):
                mm = pe.matmul(pg[:, NS * m:NS * m + NS], wxdt[:, 128 * m:128 * m + 128], wdt[:, :], start=True, stop=True)
            mm.then_inc(s_wdt, 1)
            proj(0, 1, 0, 4)
            turn_conv(0, 0)
            proj(0, 2, 0, 4, bank=py)
            turn_xn(0, 0)
            pe.wait_ge(s_wx, 1)
            token_coef(0, 0)
            turn_conv(0, 1)
            row_coef(0, 0)
            pe.wait_ge(s_sp, 1)
            pe.wait_ge(s_idb, 1)
            pe.wait_ge(s_xrb, 2)
            for n in range(T // 2):
                mm = pe.transpose(pab[:, 128 * n:128 * n + 128],
                                  spread[:, 2 * n:2 * n + 2, :].rearrange("p t j -> p (t j)"), identb[:, :])
            mm.then_inc(s_vt, 1)
            for s in range(AHEAD):
                step_product(0, 0, s)
            pe.wait_ge(s_dd, 1)
            pe.wait_ge(s_later, LATER)
            pair(0, 0)
            pair(1, 1)
            with pe.Fori(MAIN.start, MAIN.stop) as i:
                pair(i)
            pair(14, 14)
            pair(15, 15)
            y_group(15, 1, 3)
            turn_y(15, 1)
            project_out(15, 1, 0, 4)

        def conv_sum(eng, i, k):
            eng.wait_ge(s_tap, num(i, k, 1, 1))
            if from_chunk(i, k, 1):
                eng.wait_ge(s_xc, num(i, k))
            eng.tensor_tensor(conv[:, :, :], tap[0][:, :, :], tap[1][:, :, :], ALU.add).then_inc(s_cv, 1)
            for n in range(2, TAPS):
                eng.wait_ge(s_cv, num(i, k, 3, n - 1))
                eng.tensor_tensor(conv[:, :, :], conv[:, :, :], tap[n][:, :, :], ALU.add).then_inc(s_cv, 1)

        def affine(eng, i, k):
            eng.wait_ge(s_xhat, num(i, k, 1, 1))
            if from_chunk(i, k, 2):
                eng.wait_ge(s_scr[k % 2], turn(i, k, 48))
            eng.tensor_tensor(xg[:, :], xhat[:, :], gain[:, :], ALU.mult).then_inc(s_xg, 1)
            eng.wait_ge(s_xg, num(i, k, 1, 1))
            eng.tensor_tensor(xn[k % 2][:, :], xg[:, :], beta[:, :], ALU.add).then_inc(s_xn, 1)

        def residue_1(eng, i, k):
            eng.wait_ge(s_x1, num(i, k, 1, 1))
            if from_chunk(i, k, 1):
                eng.wait_ge(s_x3, num(i, k))
            eng.tensor_tensor(res[:, :], xn[k % 2][:, :], xp[0][k % 2][:, :], ALU.subtract).then_inc(s_r1, 1)

        def part_3(eng, i, k):
            eng.wait_ge(s_x2, num(i, k, 1, 1))
            if from_chunk(i, k, 2):
                eng.wait_ge(s_scr[k % 2], turn(i, k, 48))
            eng.tensor_tensor(xp[2][k % 2][:, :], res[:, :], xp[1][k % 2][:, :], ALU.subtract).then_inc(s_x3, 1)

        @block.vector
        def _(dve):
            def scan_pre(i, k, s):
                if s == 0:
                    dve.wait_ge(s_ad, num(i, k, 1, 1))
                if s >= 1 or from_chunk(i, k, 1):
                    dve.wait_ge(s_h, num(i, k, T, s))
                if s % 2 == 0:
                    dve.wait_ge(s_v, num(i, k, T, s + 2))
                dve.scalar_tensor_tensor(out=pre[:, :], in0=h[:, (s - 1) % 8, :], scalar=ad[k % 2][:, place(s):place(s) + 1],
                                         in1=pv[s % 4][:, :], op0=ALU.mult, op1=ALU.add).then_inc(s_pre, 1)

            def scan_clip(i, k, s):
                dve.wait_ge(s_pre, num(i, k, T, s + 1))
                dve.tensor_scalar(h[:, s % 8, :], pre[:, :], -CLIP, CLIP, ALU.max, ALU.min).then_inc(s_h, 1)

            def norm_stats(i, k, n):
                if n == 0:
                    dve.wait_ge(s_xct, num(i, k, 1, 1))
                    if from_chunk(i, k, 1):
                        dve.wait_ge(s_nmr, num(i, k))
                part = dve.bn_stats(stats[:, n, :], pb[:, 128 * n:128 * n + 128])
                if n == 3:
                    part.then_inc(s_st, 1)

            def norm_mean(i, k):
                made, = ready_values(dve, num(i, k, 2, 1))
                dve.wait_ge(*READY)
                dve.wait_ge(s_st, made)
                dve.bn_aggr(mv[:, :], stats[:, :, :]).then_inc(s_st, 1)

            def norm_cap(i, k):
                dve.wait_ge(s_ss, num(i, k, 1, 1))
                dve.tensor_scalar(sscap[:, :], ss[k % 2][:, :], 1.0, None, ALU.min).then_inc(s_cap, 1)

            def scale_b(i, k):
                dve.wait_ge(s_z, num(i, k, 1, 1))
                dve.wait_ge(s_ncap, num(i, k, 1, 1))
                dve.tensor_scalar(zs[:, 0:NS], pg[:, 0:NS], ncap[:, 0:1], None, ALU.mult).then_inc(s_zb, 1)

            def copy_rows(i, k):
                dve.wait_ge(s_th, num(i, k, 1, 1))
                if from_chunk(i, k, 1):
                    dve.wait_ge(s_sp, num(i, k))
                if from_chunk(i, k, 1):
                    dve.wait_ge(s_cw, num(i, k))
                dve.tensor_copy(bc[:, :, :].rearrange("p n t -> p (n t)"), pg[:, BLK:BLK + 2 * T]).then_inc(s_bc, 1)

            def gated(i, k, n):
                cols = slice(128 * n, 128 * n + 128)
                if n == 0:
                    dve.wait_ge(s_yg, num(i, k, 4, 4))
                    dve.wait_ge(s_sg, num(i, k, 1, 1))
                    if from_chunk(i, k, 1):
                        dve.wait_ge(s_yt, num(i, k))
                part = dve.tensor_tensor(yg[:, cols], py[:, cols], sg[:, cols], ALU.mult)
                if n == 3:
                    part.then_inc(s_ygs, 1)

            def residual(i, k, n):
                if n == 0:
                    dve.wait_ge(s_o, num(i, k, 1, 1))
                    if from_chunk(i, k, 2):
                        dve.wait_ge(s_out[k % 2], turn(i, k, 16))
                cols = slice(128 * n, 128 * n + 128)
                part = dve.tensor_tensor(fin[k % 2][:, cols], pg[:, OUT][:, cols], xres[k % 2][:, cols], ALU.add)
                if n == 1:
                    part.then_inc(s_fin, 1)

            def pair(i, fixed=None):
                for k in range(2):
                    c = 4 if fixed is None else 2 * fixed + k
                    for s in range(T):
                        scan_pre(i, k, s)
                        scan_clip(i, k, s)
                        if s == 0:
                            if c + 1 < NCH:
                                norm_cap(i, k + 1)
                        if s == 1:
                            if c >= 2:
                                residual(i, k - 2, 0)
                        if s == 2:
                            if c >= 2:
                                residual(i, k - 2, 1)
                            if c >= 1:
                                gated(i, k - 1, 0)
                        if s == 3:
                            if c >= 1:
                                gated(i, k - 1, 1)
                                gated(i, k - 1, 2)
                                gated(i, k - 1, 3)
                        if s == 4:
                            if c + 1 < NCH:
                                scale_b(i, k + 1)
                        if s == 5:
                            if c + 2 < NCH:
                                norm_stats(i, k + 2, 0)
                        if s == 6:
                            if c + 2 < NCH:
                                norm_stats(i, k + 2, 1)
                        if s == 7:
                            if c + 1 < NCH:
                                copy_rows(i, k + 1)
                        if s == 8:
                            if c + 2 < NCH:
                                norm_stats(i, k + 2, 2)
                        if s == 9:
                            if c + 2 < NCH:
                                norm_stats(i, k + 2, 3)
                        if s == 10:
                            if c + 2 < NCH:
                                norm_mean(i, k + 2)

            dve.memset(xrb[0][:, :, 0:HIST], 0.0).then_inc(s_zero, 1)
            dve.memset(h[:, 7, :], 0.0).then_inc(s_zero, 1)
            dve.memset(spread[:, :, :], 0.0).then_inc(s_zero, 1)
            for j in range(2):
                dve.memset(cw[j][:, :, :], 0.0).then_inc(s_zero, 1)
            conv_sum(dve, 0, 0)
            dve.wait_ge(s_const, CONST)
            dve.tensor_copy(identb[:, :], ident[:, :]).then_inc(s_idb, 1)
            for m in range(MT):
                part = dve.tensor_scalar(ddiag[:, m, :], ident[:, :], dcol[:, m:m + 1], None, ALU.mult)
            part.then_inc(s_dd, 1)
            dve.wait_ge(s_wdt, 1)
            dve.tensor_copy(wx[:, :, 2 * NS:], pg[:, 0:NS * MT].rearrange("p (m n) -> p m n", m=MT)).then_inc(s_wx, 1)
            for n in range(4):
                norm_stats(0, 0, n)
            norm_mean(0, 0)
            affine(dve, 0, 0)
            residue_1(dve, 0, 0)
            conv_sum(dve, 0, 1)
            norm_cap(0, 0)
            part_3(dve, 0, 0)
            scale_b(0, 0)
            for n in range(4):
                norm_stats(0, 1, n)
            norm_mean(0, 1)
            copy_rows(0, 0)
            affine(dve, 0, 1)
            residue_1(dve, 0, 1)
            conv_sum(dve, 0, 2)
            part_3(dve, 0, 1)
            dve.wait_ge(s_zero, 5)
            pair(0, 0)
            pair(1, 1)
            with dve.Fori(MAIN.start, MAIN.stop) as i:
                pair(i)
            pair(14, 14)
            pair(15, 15)
            residual(15, 0, 0)
            residual(15, 0, 1)
            for n in range(4):
                gated(15, 1, n)
            residual(15, 1, 0)
            residual(15, 1, 1)

        @block.scalar
        def _(act):
            def proj_out(i, k, bank=pa):
                act.wait_ge(s_xr, num(i, k, 1, 1))
                product = bank[:, :].rearrange("p (m n) -> p m n", m=MT)
                act.activation(xrb[k % 2][:, :, HIST:], product, ACT.Copy)
                act.activation(xrb[(k + 1) % 2][:, :, 0:HIST], product[:, :, 128 - HIST:], ACT.Copy).then_inc(s_xrb, 1)

            def conv_taps(i, k, first, last):
                if first == 0:
                    act.wait_ge(s_xrb, num(i, k, 1, 1))
                    if from_chunk(i, k, 1):
                        act.wait_ge(s_cv, num(i, k, 3))
                for n in range(first, last):
                    for m in range(MT):
                        a = act.activation(tap[n][:, m, :], xrb[k % 2][:, m, NB * n:NB * n + 128], ACT.Copy,
                                           scale=wconv[:, m, n:n + 1])
                if last == TAPS:
                    a.then_inc(s_tap, 1)

            def conv_silu(i, k):
                act.wait_ge(s_cv, num(i, k, 3, 3))
                if from_chunk(i, k, 2):
                    act.wait_ge(s_xct, num(i, k, 1, -1))
                for m in range(MT):
                    a = act.activation(xc[k % 2][:, m, :].rearrange("p (q r b) -> p q r b", q=4, r=4),
                                       conv[:, m, :].rearrange("p (r q b) -> p q r b", q=4, r=4), ACT.Silu,
                                       bias=bconv[:, m:m + 1])
                a.then_inc(s_xc, 1)

            def normalise(i, k):
                act.wait_ge(s_nmr, num(i, k, 1, 1))
                if from_chunk(i, k, 1):
                    act.wait_ge(s_xg, num(i, k))
                act.activation(xhat[:, :], pb[:, :], ACT.Identity, bias=nmr[:, 0:1], scale=rstd[:, 0:1]
                               ).then_inc(s_xhat, 1)

            def part_1(i, k):
                act.wait_ge(s_xn, num(i, k, 1, 1))
                if from_chunk(i, k, 2):
                    act.wait_ge(s_scr[k % 2], turn(i, k, 48))
                act.activation(xp[0][k % 2][:, :], xn[k % 2][:, :], ACT.Copy).then_inc(s_x1, 1)

            def square(i, k):
                if from_chunk(i, k, 2):
                    act.wait_ge(s_cap, num(i, k, 1, -1))
                act.activation(sq[:, :], xn[k % 2][:, :], ACT.Square, accum_out=ss[k % 2][:, :]).then_inc(s_ss, 1)

            def part_2(i, k):
                act.wait_ge(s_r1, num(i, k, 1, 1))
                act.activation(xp[1][k % 2][:, :], res[:, :], ACT.Copy).then_inc(s_x2, 1)

            def xn_by_channel(i, k):
                act.wait_ge(s_xnt, num(i, k, 1, 1))
                if from_chunk(i, k, 2):
                    act.wait_ge(s_dx, num(i, k, 1, -1))
                act.activation(xnT[k % 2][:, :, :].rearrange("p m n -> p (m n)"), pb[:, :], ACT.Copy).then_inc(s_xnts, 1)

            def copy_c_dt(i, k):
                act.wait_ge(s_zb, num(i, k, 1, 1))
                if from_chunk(i, k, 1):
                    act.wait_ge(s_zx, num(i, k, 3))
                act.activation(zs[:, NS:], pg[:, NS:3 * NS], ACT.Copy).then_inc(s_zc, 1)

            def tanh_dt(i, k):
                act.wait_ge(s_blk, num(i, k, 1, 1))
                if from_chunk(i, k, 1):
                    act.wait_ge(s_ad, num(i, k))
                act.activation(th[:, :], pg[:, BLK + 2 * T:BLK + 3 * T], ACT.Tanh, bias=bdt[:, 0:1]).then_inc(s_th, 1)

            def bd_parts_out(i, k):
                act.wait_ge(s_vt, num(i, k, 1, 1))
                if from_chunk(i, k, 2):
                    act.wait_ge(s_v, num(i, k, T, -T))
                act.activation(vw[k % 2][:, :, :].rearrange("p n m -> p (n m)"), pab[:, :], ACT.Copy).then_inc(s_vw, 1)

            def gate_silu(i, k):
                act.wait_ge(s_gate, num(i, k, 1, 1))
                if from_chunk(i, k, 1):
                    act.wait_ge(s_ygs, num(i, k))
                act.activation(sg[:, :], pg[:, :], ACT.Silu).then_inc(s_sg, 1)

            def y_by_channel(i, k):
                act.wait_ge(s_yt, num(i, k, 1, 1))
                if from_chunk(i, k, 1):
                    act.wait_ge(s_o, num(i, k))
                act.activation(ygT[:, :, :].rearrange("p m n -> p (m n)"), pb[:, :], ACT.Copy).then_inc(s_yts, 1)

            def pair(i, fixed=None):
                for k in range(2):
                    c = 4 if fixed is None else 2 * fixed + k
                    if c + 1 < NCH:
                        xn_by_channel(i, k + 1)
                    if c + 2 < NCH:
                        conv_silu(i, k + 2)
                    if c + 1 < NCH:
                        copy_c_dt(i, k + 1)
                        tanh_dt(i, k + 1)
                    if c + 3 < NCH:
                        proj_out(i, k + 3)
                        conv_taps(i, k + 3, 0, 1)
                        conv_taps(i, k + 3, 1, 2)
                    if c + 2 < NCH:
                        normalise(i, k + 2)
                    if c + 1 < NCH:
                        bd_parts_out(i, k + 1)
                    if c + 3 < NCH:
                        conv_taps(i, k + 3, 2, 3)
                    gate_silu(i, k)
                    if c + 2 < NCH:
                        part_1(i, k + 2)
                        square(i, k + 2)
                    if c >= 1:
                        y_by_channel(i, k - 1)
                    if c + 3 < NCH:
                        conv_taps(i, k + 3, 3, TAPS)
                    if c + 2 < NCH:
                        part_2(i, k + 2)

            act.wait_ge(s_zero, 1)
            act.activation(sg[:, 0:HIST], xrb[0][:, 0, 0:HIST], ACT.Silu)
            act.wait_ge(s_first, FIRST)
            proj_out(0, 0)
            conv_taps(0, 0, 0, TAPS)
            act.wait_ge(s_const, CONST)
            act.activation(acol[:, :], alog[:, :], ACT.Tanh).then_inc(s_acol, 1)
            conv_silu(0, 0)
            proj_out(0, 1)
            conv_taps(0, 1, 0, 3)
            normalise(0, 0)
            conv_taps(0, 1, 3, TAPS)
            part_1(0, 0)
            xn_by_channel(0, 0)
            square(0, 0)
            part_2(0, 0)
            proj_out(0, 2, bank=py)
            conv_silu(0, 1)
            copy_c_dt(0, 0)
            conv_taps(0, 2, 0, 2)
            tanh_dt(0, 0)
            normalise(0, 1)
            conv_taps(0, 2, 2, 3)
            part_1(0, 1)
            square(0, 1)
            conv_taps(0, 2, 3, TAPS)
            bd_parts_out(0, 0)
            part_2(0, 1)
            pair(0, 0)
            pair(1, 1)
            with act.Fori(MAIN.start, MAIN.stop) as i:
                pair(i)
            pair(14, 14)
            pair(15, 15)
            y_by_channel(15, 1)

        @block.gpsimd
        def _(pool):
            def norm_root(i, k):
                made, = ready_values(pool, num(i, k, 2, 2))
                pool.wait_ge(*READY)
                pool.wait_ge(s_st, made)
                pool.tensor_scalar(vare[:, :], mv[:, 1:2], 1e-5, None, ALU.add).then_inc(s_vare, 1)
                if from_chunk(i, k, 1):
                    pool.wait_ge(s_xhat, num(i, k))
                pool.wait_ge(s_vare, num(i, k, 1, 1))
                pool.tensor_tensor(rstd[:, :], vare[:, :], expo[:, 0:1], ALU.pow).then_inc(s_rstd, 1)
                made, = ready_values(pool, num(i, k, 1, 1))
                pool.wait_ge(*READY)
                pool.wait_ge(s_rstd, made)
                pool.tensor_scalar(nmr[:, :], mv[:, 0:1], rstd[:, 0:1], -1.0, ALU.mult, ALU.mult).then_inc(s_nmr, 1)

            def cap_root(i, k):
                pool.wait_ge(s_cap, num(i, k, 1, 1))
                if from_chunk(i, k, 1):
                    pool.wait_ge(s_zb, num(i, k))
                pool.tensor_tensor(ncap[:, :], sscap[:, :], expo[:, 1:2], ALU.pow).then_inc(s_ncap, 1)

            def spread_tokens(i, k):
                pool.wait_ge(s_zb, num(i, k, 1, 1))
                pool.wait_ge(s_zc, num(i, k, 1, 1))
                if from_chunk(i, k, 1):
                    pool.wait_ge(s_blk, num(i, k))
                for n in range(3):
                    pool.tensor_tensor(zx[:, n, :, :], bcast(zs[:, NS * n:NS * n + NS], 1, NB),
                                       bcast(tokmask[:, :], 2, NS), ALU.mult).then_inc(s_zx, 1)

            def decay(i, k):
                made, read = ready_values(pool, num(i, k, 1, 1), num(i, k, T, -T))
                pool.wait_ge(*READY)
                pool.wait_ge(s_th, made)
                if from_chunk(i, k, 2):
                    pool.wait_ge(s_pre, read)
                pool.tensor_scalar(ad[k % 2][:, :], th[:, :], acol[:, 0:1], 1.0, ALU.mult, ALU.add).then_inc(s_ad, 1)

            def bd_parts(i, k):
                made, = ready_values(pool, num(i, k, 1, 1))
                pool.wait_ge(*READY)
                pool.wait_ge(s_bc, made)
                pool.tensor_copy(bp[0][:, :], bc[:, 0, :]).then_inc(s_bp, 1)
                pool.wait_ge(s_bp, num(i, k, 4, 1))
                pool.tensor_tensor(bres[:, :], bc[:, 0, :], bp[0][:, :], ALU.subtract).then_inc(s_bp, 1)
                made, = ready_values(pool, num(i, k, 4, 2))
                pool.wait_ge(*READY)
                pool.wait_ge(s_bp, made)
                pool.tensor_copy(bp[1][:, :], bres[:, :]).then_inc(s_bp, 1)
                pool.wait_ge(s_bp, num(i, k, 4, 3))
                pool.tensor_tensor(bp[2][:, :], bres[:, :], bp[1][:, :], ALU.subtract).then_inc(s_bp, 1)

            def spread_rows(i, k):
                pool.wait_ge(s_bp, num(i, k, 4, 4))
                if from_chunk(i, k, 1):
                    pool.wait_ge(s_vt, num(i, k))
                for n, p in enumerate(BPART):
                    last = pool.tensor_tensor(spread[:, :, NB * n:NB * n + NB], bcast(bp[p][:, :], 2, NB),
                                              bcast(rowmask[:, :], 1, T), ALU.mult)
                last.then_inc(s_sp, 1)
                if from_chunk(i, k, 2):
                    pool.wait_ge(s_yg, num(i, k, 4, -4))
                for odd in range(2):
                    last = pool.tensor_tensor(
                        cw[k % 2][:, :, 0:128].rearrange("p r (q n) -> p r q n", q=2)[:, :, :, 32 * odd:32 * odd + NB],
                        bcast(bc[:, 1, 8 * odd:8 * odd + 8].rearrange("p (r q) -> p r q", r=4), 3, NB),
                        bcast(bcast(rowmask[:, :], 1, 2), 1, 4), ALU.mult)
                last.then_inc(s_cw, 1)

            def pair(i, fixed=None):
                for k in range(2):
                    c = 4 if fixed is None else 2 * fixed + k
                    if c + 1 < NCH:
                        cap_root(i, k + 1)
                    if c >= 1 and c + 1 < NCH:
                        part_3(pool, i, k + 1)
                    if c + 1 < NCH:
                        spread_tokens(i, k + 1)
                        decay(i, k + 1)
                        bd_parts(i, k + 1)
                        spread_rows(i, k + 1)
                    if c + 2 < NCH:
                        norm_root(i, k + 2)
                        affine(pool, i, k + 2)
                        residue_1(pool, i, k + 2)
                    if c + 3 < NCH:
                        conv_sum(pool, i, k + 3)

            pool.wait_ge(s_zero, 5)
            pool.wait_ge(s_const, CONST)
            pool.wait_ge(s_acol, 1)
            pool.tensor_scalar(acol[:, :], acol[:, :], -0.01, None, ALU.mult).then_inc(s_acol, 1)
            pool.wait_ge(s_acol, 2)
            norm_root(0, 0)
            cap_root(0, 0)
            spread_tokens(0, 0)
            norm_root(0, 1)
            decay(0, 0)
            bd_parts(0, 0)
            spread_rows(0, 0)
            pair(0, 0)
            pair(1, 1)
            with pool.Fori(MAIN.start, MAIN.stop) as i:
                pair(i)
            pair(14, 14)
            pair(15, 15)


def host_layout(a):
    def turned(w, tiles):
        return np.ascontiguousarray(w.T.reshape(tiles, 128, w.shape[0]).transpose(1, 0, 2))

    def per_channel(w):
        return np.ascontiguousarray(w.reshape(MT, 128, -1).transpose(1, 0, 2))

    def on_all(v):
        return np.ascontiguousarray(np.broadcast_to(v[None, :], (128, v.shape[0])))

    def on_rows(v):
        return np.ascontiguousarray(np.broadcast_to(v[None, :], (NB, NS)).reshape(128, 1))

    x = np.ascontiguousarray(a["x"].reshape(NB, NCH, 4, 4, DM).transpose(1, 3, 2, 0, 4).reshape(NCH, 128, DM))
    xT = np.ascontiguousarray(x.reshape(NCH, 128, KT, 128).transpose(0, 3, 2, 1))
    p = np.arange(128)
    column = 2 * (p // 8 % 8) + p // 64
    f = np.float32
    pre = "L0_cond_"
    return {
        "x": x, "xT": xT, "w_in": turned(a[pre + "W_in"], KT), "w_out": turned(a[pre + "W_out"], MT),
        "w_xp": turned(a[pre + "W_xproj"], MT), "w_xdt": np.ascontiguousarray(a[pre + "W_xproj"][2 * NS:]),
        "w_dt": np.ascontiguousarray(a[pre + "W_dt"].T), "cond": np.ascontiguousarray(a["cond_2048"]),
        "ind8": (p[None, :] % NB == np.arange(NB)[:, None]).astype(f),
        "w_conv": per_channel(a[pre + "W_conv"]), "b_conv": per_channel(a[pre + "b_conv"])[:, :, 0].copy(),
        "gain": on_all(a[pre + "ln_g"]), "beta": on_all(a[pre + "ln_b"]), "dcol": per_channel(a[pre + "D"])[:, :, 0].copy(),
        "alog": on_rows(a[pre + "A_log"]), "b_dt": on_rows(a[pre + "b_dt"]), "ident": np.eye(128, dtype=f),
        "rowmask": (p[:, None] // NS == np.arange(NB)[None, :]).astype(f),
        "tokmask": (p[:, None] % NB == np.arange(NB)[None, :]).astype(f),
        "tsel": (column[:, None] == np.arange(T)[None, :]).astype(f),
        "expo": np.ascontiguousarray(np.broadcast_to(np.array([-0.5, 0.5], f), (128, 2))),
    }


def declare(nc, arrays):
    d = {n: nc.dram_tensor(f"in_{n}", v.shape, F32, kind="ExternalInput").ap() for n, v in arrays.items()}
    d["out"] = nc.dram_tensor("out_0", (NCH, 128, DM), F32, kind="ExternalOutput").ap()
    return d


def kernel(**inputs):
    import concourse.bacc as _bacc
    from concourse.bass_utils import run_bass_kernel_spmd as run

    arrays = host_layout({k: np.asarray(v) for k, v in inputs.items()})
    nc = _bacc.Bacc("TRN2", target_bir_lowering=False, num_devices=1)
    build(nc, declare(nc, arrays))
    r = run(nc, [{f"in_{n}": v for n, v in arrays.items()}], core_ids=[0])
    out = r.results[0]["out_0"].reshape(NCH, 4, 4, NB, DM)
    return np.ascontiguousarray(out.transpose(3, 0, 2, 1, 4).reshape(NB, SEQ, DM))
```

```python
from contextlib import ExitStack

import numpy as np

import concourse.bass as bass
from concourse import mybir

F32 = mybir.dt.float32
BF16 = mybir.dt.bfloat16
ALU = mybir.AluOpType
ACT = mybir.ActivationFunctionType

NB, SEQ, DM = 8, 512, 256
DI, NS = 512, 16
T = 16
NCH = SEQ // T
TAPS = 4
MT, KT = DI // 128, DM // 128
HIST = (TAPS - 1) * NB
CLIP = 10.0
XPART = (0, 0, 0, 1, 1, 2)
BPART = (0, 1, 2, 0, 1, 0)
NJ = len(XPART)
KV = NJ * NB
AHEAD = 3
MAIN = range(2, 14)


def from_chunk(i, k, first):
    return not isinstance(i, int) or 2 * i + k >= first


def ready_values(eng, *values):
    for value in values:
        if not isinstance(value, int):
            eng.compute_val(value)
    return values


def place(s):
    q, r = s % 4, s // 4
    return 8 * (q % 2) + 2 * r + q // 2


def bcast(ap, axis, n):
    ap = ap.unsqueeze(axis)
    shape = list(ap.shape)
    shape[axis] = n
    return ap.to_broadcast(shape)


def build(nc, d):
    with ExitStack() as ctx:
        def sb(name, shape, dt=F32):
            return ctx.enter_context(nc.sbuf_tensor(name, shape, dt))

        def psum(name):
            return ctx.enter_context(nc.psum_tensor(name, [128, 512], F32))

        def sem(name):
            return ctx.enter_context(nc.semaphore(name))

        xp_dram = nc.dram_tensor("xp_scratch", (3, 2, NCH, NB, T // 2, DI), BF16, kind="Internal").ap()

        win = sb("win", [128, KT, 2 * DI])
        wout = sb("wout", [128, MT, DM])
        wx = sb("wx", [128, MT, 3 * NS])
        wxdt = sb("wxdt", [NS, DI])
        wdt = sb("wdt", [NS, NS])
        cond = sb("cond", [NB, DI])
        ind8 = sb("ind8", [NB, 128])
        wconv = sb("wconv", [128, MT, TAPS])
        bconv = sb("bconv", [128, MT])
        gain = sb("gain", [128, DI])
        beta = sb("beta", [128, DI])
        dcol = sb("dcol", [128, MT])
        ddiag = sb("ddiag", [128, MT, 128])
        alog = sb("alog", [128, 1])
        acol = sb("acol", [128, 1])
        bdt = sb("bdt", [128, 1])
        ident = sb("ident", [128, 128])
        identb = sb("identb", [128, 128], BF16)
        rowmask = sb("rowmask", [128, NB])
        tokmask = sb("tokmask", [128, NB])
        tsel = sb("tsel", [128, T])
        expo = sb("expo", [128, 2])

        xt = [sb(f"xt{j}", [128, KT, 128]) for j in range(2)]
        xrb = [sb(f"xrb{j}", [128, MT, HIST + 128]) for j in range(2)]
        conv = sb("conv", [128, MT, 128])
        tap = [sb(f"tap{n}", [128, MT, 128]) for n in range(TAPS)]
        xc = [sb(f"xc{j}", [128, MT, 128]) for j in range(2)]
        stats = sb("stats", [128, 4, 6])
        mv = sb("mv", [128, 2])
        vare = sb("vare", [128, 1])
        rstd = sb("rstd", [128, 1])
        nmr = sb("nmr", [128, 1])
        xhat = sb("xhat", [128, DI])
        xg = sb("xg", [128, DI])
        xn = [sb(f"xn{j}", [128, DI]) for j in range(2)]
        sq = sb("sq", [128, DI])
        ss = [sb(f"ss{j}", [128, 1]) for j in range(2)]
        res = sb("res", [128, DI])
        xp = [[sb(f"xp{p}_{j}", [128, DI], BF16) for j in range(2)] for p in range(3)]
        xnT = [sb(f"xnT{j}", [128, MT, 128]) for j in range(2)]
        sscap = sb("sscap", [128, 1])
        ncap = sb("ncap", [128, 1])
        zs = sb("zs", [128, 3 * NS])
        zx = sb("zx", [128, 3, NB, NS])
        th = sb("th", [128, T])
        bc = sb("bc", [128, 2, T])
        bres = sb("bres", [128, T])
        bp = [sb(f"bp{p}", [128, T], BF16) for p in range(3)]
        spread = sb("spread", [128, T, 64], BF16)
        ad = [sb(f"ad{j}", [128, T]) for j in range(2)]
        vw = [sb(f"vw{j}", [128, T // 2, 128], BF16) for j in range(2)]
        cw = [sb(f"cw{j}", [128, 4, 136]) for j in range(2)]
        xr = [sb(f"xr{j}", [128, T // 2, DI], BF16) for j in range(2)]
        pre = sb("pre", [128, DI])
        h = sb("h", [128, 8, DI])
        xtb = [sb(f"xtb{j}", [128, KT, 128]) for j in range(2)]
        sg = sb("sg", [128, DI])
        yg = sb("yg", [128, DI])
        ygT = sb("ygT", [128, MT, 128])
        fin = [sb(f"fin{j}", [128, DM]) for j in range(2)]

        pv = [psum(f"pv{j}") for j in range(4)]
        py = psum("py")
        pa = psum("pa")
        pb = psum("pb")
        pg = psum("pg")
        pab = pa[:, :].bitcast(BF16)
        Z, BLK, OUT = slice(0, 48), 64, slice(256, 512)

        s_first = sem("s_first")
        s_const = sem("s_const")
        s_later = sem("s_later")
        s_zero = sem("s_zero")
        s_wdt = sem("s_wdt")
        s_wx = sem("s_wx")
        s_acol = sem("s_acol")
        s_idb = sem("s_idb")
        s_xt = [sem(f"s_xt{j}") for j in range(2)]
        s_xr = sem("s_xr")
        s_xrb = sem("s_xrb")
        s_tap = sem("s_tap")
        s_cv = sem("s_cv")
        s_xc = sem("s_xc")
        s_xct = sem("s_xct")
        s_st = sem("s_st")
        s_vare = sem("s_vare")
        s_rstd = sem("s_rstd")
        s_nmr = sem("s_nmr")
        s_xhat = sem("s_xhat")
        s_xg = sem("s_xg")
        s_xn = sem("s_xn")
        s_ss = sem("s_ss")
        s_x1 = sem("s_x1")
        s_r1 = sem("s_r1")
        s_x2 = sem("s_x2")
        s_x3 = sem("s_x3")
        s_scr = [sem(f"s_scr{j}") for j in range(2)]
        s_xp = [sem(f"s_xp{j}") for j in range(2)]
        s_xnt = sem("s_xnt")
        s_xnts = sem("s_xnts")
        s_cap = sem("s_cap")
        s_ncap = sem("s_ncap")
        s_z = sem("s_z")
        s_zs = sem("s_zs")
        s_zx = sem("s_zx")
        s_blk = sem("s_blk")
        s_th = sem("s_th")
        s_bc = sem("s_bc")
        s_ad = sem("s_ad")
        s_bp = sem("s_bp")
        s_sp = sem("s_sp")
        s_cw = sem("s_cw")
        s_vt = sem("s_vt")
        s_vw = sem("s_vw")
        s_v = sem("s_v")
        s_pre = sem("s_pre")
        s_h = sem("s_h")
        s_yg = sem("s_yg")
        s_bk = [sem(f"s_bk{j}") for j in range(2)]
        s_gate = sem("s_gate")
        s_sg = sem("s_sg")
        s_dd = sem("s_dd")
        s_dx = sem("s_dx")
        s_ygs = sem("s_ygs")
        s_yt = sem("s_yt")
        s_yts = sem("s_yts")
        s_o = sem("s_o")
        s_fin = sem("s_fin")
        s_out = [sem(f"s_out{j}") for j in range(2)]

        first = [(win[:, :, 0:DI], d["w_in"][:, :, 0:DI]), (cond[:, :], d["cond"]), (ind8[:, :], d["ind8"]),
                 (wconv[:, :, :], d["w_conv"])]
        consts = [(bconv[:, :], d["b_conv"]), (ident[:, :], d["ident"]), (expo[:, :], d["expo"]),
                  (gain[:, :], d["gain"]), (beta[:, :], d["beta"]), (wxdt[:, :], d["w_xdt"]), (wdt[:, :], d["w_dt"]),
                  (wx[:, :, :], d["w_xp"]), (tokmask[:, :], d["tokmask"]), (tsel[:, :], d["tsel"]),
                  (bdt[:, :], d["b_dt"]), (alog[:, :], d["alog"]), (rowmask[:, :], d["rowmask"]),
                  (dcol[:, :], d["dcol"])]
        later = [(win[:, :, DI:2 * DI], d["w_in"][:, :, DI:2 * DI]), (wout[:, :, :], d["w_out"])]
        FIRST, CONST, LATER = (16 * len(group) for group in (first, consts, later))
        READY = (s_first, FIRST)

        def num(i, k, per=1, more=0):
            return i * (2 * per) + (per * k + more)

        def turn(i, k, per=1, more=0):
            return i * per + (per * (k // 2) + more)

        def stage(i, k, ahead):
            return min(2 * i + k + ahead, NCH) if isinstance(i, int) else num(i, k, 1, ahead)

        block = ctx.enter_context(nc.Block())

        @block.sync
        def _(sp):
            def load_xt(i, k):
                if from_chunk(i, k, 2):
                    read, = ready_values(sp, num(i, k, 1, -1))
                    sp.wait_ge(*READY)
                    sp.wait_ge(s_xr, read)
                sp.dma_start(xt[k % 2][:, :, :], d["xT"][bass.ds(num(i, k), 1)].rearrange("o p k n -> (o p) k n")
                             ).then_inc(s_xt[k % 2], 16)

            def store_scratch(i, k):
                j = k % 2
                for p, ready in enumerate((s_x1, s_x2, s_x3)):
                    made, = ready_values(sp, num(i, k, 1, 1))
                    sp.wait_ge(*READY)
                    sp.wait_ge(ready, made)
                    for e in range(2):
                        sp.dma_start(xp_dram[p, e][bass.ds(num(i, k), 1)].rearrange("o b f n -> (o f) b n"),
                                     xp[p][j][64 * e:64 * e + 64, :]).then_inc(s_scr[j], 16)

            def load_xr(i, k):
                j = k % 2
                stored, read = ready_values(sp, turn(i, k, 96, 96), num(i, k, T, -T))
                sp.wait_ge(*READY)
                sp.wait_ge(s_scr[j], stored)
                if from_chunk(i, k, 2):
                    sp.wait_ge(s_v, read)
                for p in range(3):
                    copies = XPART.count(p)
                    for e in range(2):
                        row = 64 * e + NB * XPART.index(p)
                        part = xp_dram[p, e][bass.ds(num(i, k), 1)].rearrange("o b f n -> (o b) (f n)")
                        sp.dma_start(xr[j][row:row + NB * copies, :, :], bcast(part, 0, copies)).then_inc(s_xp[j], 16)

            def load_back(i, k):
                j = k % 2
                if from_chunk(i, k, 2):
                    read, = ready_values(sp, num(i, k, 1, -1))
                    sp.wait_ge(*READY)
                    sp.wait_ge(s_o, read)
                c = bass.ds(num(i, k), 1)
                sp.dma_start(xtb[j][:, :, :], d["xT"][c].rearrange("o p k n -> (o p) k n")).then_inc(s_bk[j], 16)

            def store_out(i, k):
                made, = ready_values(sp, num(i, k, 1, 1))
                sp.wait_ge(*READY)
                sp.wait_ge(s_fin, made)
                sp.dma_start(d["out"][bass.ds(num(i, k), 1)].rearrange("o p n -> (o p) n"), fin[k % 2][:, :]
                             ).then_inc(s_out[k % 2], 16)

            def pair(i, fixed=None):
                for k in range(2):
                    c = 4 if fixed is None else 2 * fixed + k
                    if c >= 2:
                        store_out(i, k - 2)
                    load_back(i, k)
                    if c + 1 < NCH:
                        load_xr(i, k + 1)
                    if c + 4 < NCH:
                        load_xt(i, k + 4)
                    if c + 2 < NCH:
                        store_scratch(i, k + 2)

            load_xt(0, 0)
            for dst, src in first:
                sp.dma_start(dst, src).then_inc(s_first, 16)
            for dst, src in consts:
                sp.dma_start(dst, src).then_inc(s_const, 16)
            load_xt(0, 1)
            for dst, src in later:
                sp.dma_start(dst, src).then_inc(s_later, 16)
            load_xt(0, 2)
            store_scratch(0, 0)
            load_xr(0, 0)
            load_xt(0, 3)
            store_scratch(0, 1)
            pair(0, 0)
            pair(1, 1)
            with sp.Fori(MAIN.start, MAIN.stop) as i:
                pair(i)
            pair(14, 14)
            pair(15, 15)
            store_out(15, 0)
            store_out(15, 1)
            for j in range(2):
                sp.wait_ge(s_out[j], 16 * NCH // 2)

        @block.tensor
        def _(pe):
            def step_product(i, k, s):
                j, slot, row = k % 2, place(s) // 2, 64 * (place(s) % 2)
                if s == 0:
                    pe.wait_ge(s_vw, num(i, k, 1, 1))
                    pe.wait_ge(s_xp[j], turn(i, k, 96, 96))
                if s >= 4 or from_chunk(i, k, 1):
                    pe.wait_ge(s_pre, num(i, k, T, s - 3))
                pe.matmul(pv[s % 4][:, :], vw[j][row:row + KV, slot, :], xr[j][row:row + KV, slot, :],
                          start=True, stop=True).then_inc(s_v, 1)

            def skip(i, k):
                if from_chunk(i, k, 1):
                    pe.wait_ge(s_ygs, num(i, k))
                for m in range(MT):
                    mm = pe.matmul(py[:, 128 * m:128 * m + 128], xnT[k % 2][:, m, :], ddiag[:, m, :],
                                   start=(m == 0), stop=False)
                mm.then_inc(s_dx, 1)

            def y_group(i, k, r):
                if r == 0:
                    pe.wait_ge(s_cw, num(i, k, 1, 1))
                pe.wait_ge(s_h, num(i, k, T, 4 * r + 4))
                for q in range(4):
                    mm = pe.matmul(py[32 * q:32 * q + 32, :], c_of(k % 2)[:, 128 * r + 32 * q:128 * r + 32 * q + 32],
                                   h[:, (4 * r + q) % 8, :], start=False, stop=(r == 3),
                                   tile_position=(0, 32 * q))
                mm.then_inc(s_yg, 1)

            def c_of(j):
                return cw[j][:, :, :].rearrange("p r n -> p (r n)")

            def proj(i, k, m0, m1, bank=pa):
                if m0 == 0:
                    pe.wait_ge(s_xt[k % 2], turn(i, k, 16, 16))
                    if from_chunk(i, k, 3):
                        pe.wait_ge(s_vw, num(i, k, 1, -2))
                    if from_chunk(i, k, 1):
                        pe.wait_ge(s_xrb, num(i, k))
                for m in range(m0, m1):
                    for kt in range(KT):
                        pe.matmul(bank[:, 128 * m:128 * m + 128], win[:, kt, 128 * m:128 * m + 128],
                                  xt[k % 2][:, kt, :].rearrange("p (q r b) -> p r q b", q=4, r=4),
                                  start=(kt == 0), stop=False)
                    mm = pe.matmul(bank[:, 128 * m:128 * m + 128], cond[:, 128 * m:128 * m + 128], ind8[:, :],
                                   start=False, stop=True)
                if m1 == MT:
                    mm.then_inc(s_xr, 1)

            def turn_conv(i, k):
                pe.wait_ge(s_xc, num(i, k, 1, 1))
                if from_chunk(i, k, 2):
                    pe.wait_ge(s_xnts, num(i, k, 1, -1))
                if from_chunk(i, k, 4):
                    pe.wait_ge(s_yts, num(i, k, 1, -3))
                for m in range(MT):
                    mm = pe.transpose(pb[:, 128 * m:128 * m + 128], xc[k % 2][:, m, :], ident[:, :])
                mm.then_inc(s_xct, 1)

            def turn_xn(i, k):
                pe.wait_ge(s_xn, num(i, k, 1, 1))
                pe.wait_ge(s_xhat, num(i, k, 1, 1))
                if from_chunk(i, k, 3):
                    pe.wait_ge(s_yts, num(i, k, 1, -2))
                for m in range(MT):
                    mm = pe.transpose(pb[:, 128 * m:128 * m + 128], xn[k % 2][:, 128 * m:128 * m + 128], ident[:, :])
                mm.then_inc(s_xnt, 1)

            def token_coef(i, k):
                pe.wait_ge(s_xnts, num(i, k, 1, 1))
                if from_chunk(i, k, 3):
                    pe.wait_ge(s_fin, num(i, k, 1, -2))
                for m in range(MT):
                    mm = pe.matmul(pg[:, Z], xnT[k % 2][:, m, :], wx[:, m, :], start=(m == 0), stop=(m == MT - 1))
                mm.then_inc(s_z, 1)

            def row_coef(i, k):
                pe.wait_ge(s_zx, num(i, k, 3, 3))
                for n in range(3):
                    mm = pe.matmul(pg[:, BLK + T * n:BLK + T * n + T], zx[:, n, :, :].rearrange("p b s -> p (b s)"),
                                   tsel[:, :], start=True, stop=True)
                mm.then_inc(s_blk, 1)

            def turn_spread(i, k):
                pe.wait_ge(s_sp, num(i, k, 1, 1))
                pe.wait_ge(s_xrb, stage(i, k, 3))
                for n in range(T // 2):
                    mm = pe.transpose(pab[:, 128 * n:128 * n + 128],
                                      spread[:, 2 * n:2 * n + 2, :].rearrange("p t j -> p (t j)"), identb[:, :])
                mm.then_inc(s_vt, 1)

            def gate(i, k, n):
                half, kt = n // KT, n % KT
                cols = slice(256 * half, 256 * half + 256)
                if n == 0:
                    pe.wait_ge(s_bk[k % 2], turn(i, k, 16, 16))
                    if from_chunk(i, k, 2):
                        pe.wait_ge(s_fin, num(i, k, 1, -1))
                    pe.wait_ge(s_th, stage(i, k, 2))
                    pe.wait_ge(s_bc, stage(i, k, 2))
                mm = pe.matmul(pg[:, cols], xtb[k % 2][:, kt, :], win[:, kt, DI:][:, cols],
                               start=(kt == 0), stop=(kt == KT - 1))
                if n == 3:
                    mm.then_inc(s_gate, 1)

            def turn_y(i, k):
                pe.wait_ge(s_ygs, num(i, k, 1, 1))
                pe.wait_ge(s_xhat, stage(i, k, 4))
                for m in range(MT):
                    mm = pe.transpose(pb[:, 128 * m:128 * m + 128], yg[:, 128 * m:128 * m + 128], ident[:, :])
                mm.then_inc(s_yt, 1)

            def project_out(i, k, m0, m1):
                if m0 == 0:
                    pe.wait_ge(s_yts, num(i, k, 1, 1))
                    pe.wait_ge(s_sg, stage(i, k, 2))
                    if from_chunk(i, k, 1):
                        pe.wait_ge(s_fin, num(i, k))
                    for kt in range(KT):
                        pe.matmul(pg[:, OUT][:, 128 * kt:128 * kt + 128], xtb[k % 2][:, kt, :], ident[:, :],
                                  start=(kt == 0), stop=False)
                for m in range(m0, m1):
                    mm = pe.matmul(pg[:, OUT], ygT[:, m, :], wout[:, m, :], start=False, stop=(m == MT - 1))
                if m1 == MT:
                    mm.then_inc(s_o, 1)

            def pair(i, fixed=None):
                for k in range(2):
                    c = 4 if fixed is None else 2 * fixed + k
                    for s in range(T):
                        if s + AHEAD < T:
                            step_product(i, k, s + AHEAD)
                        elif c + 1 < NCH:
                            step_product(i, k + 1, s + AHEAD - T)
                        if s == 0:
                            if c >= 1:
                                y_group(i, k - 1, 3)
                            if c + 3 < NCH:
                                proj(i, k + 3, 0, 1)
                            if c >= 2:
                                project_out(i, k - 2, 2, 4)
                        if s == 1:
                            if c + 1 < NCH:
                                turn_xn(i, k + 1)
                        if s == 2:
                            if c + 3 < NCH:
                                proj(i, k + 3, 1, 2)
                        if s == 3:
                            if c + 1 < NCH:
                                token_coef(i, k + 1)
                        if s == 4:
                            if c + 3 < NCH:
                                proj(i, k + 3, 2, 3)
                        if s == 5:
                            if c + 2 < NCH:
                                turn_conv(i, k + 2)
                            skip(i, k)
                            if c + 1 < NCH:
                                row_coef(i, k + 1)
                            y_group(i, k, 0)
                        if s == 8:
                            if c + 3 < NCH:
                                proj(i, k + 3, 3, 4)
                        if s == 9:
                            y_group(i, k, 1)
                            if c + 1 < NCH:
                                turn_spread(i, k + 1)
                        if s == 10:
                            gate(i, k, 0)
                            gate(i, k, 1)
                        if s == 11:
                            y_group(i, k, 2)
                        if s == 12:
                            gate(i, k, 2)
                            gate(i, k, 3)
                        if s == 13:
                            if c >= 1:
                                turn_y(i, k - 1)
                        if s == 14:
                            if c >= 1:
                                project_out(i, k - 1, 0, 2)

            pe.wait_ge(s_first, FIRST)
            proj(0, 0, 0, 4)
            pe.wait_ge(s_const, CONST)
            for m in range(MT):
                mm = pe.matmul(pg[:, NS * m:NS * m + NS], wxdt[:, 128 * m:128 * m + 128], wdt[:, :], start=True, stop=True)
            mm.then_inc(s_wdt, 1)
            proj(0, 1, 0, 4)
            turn_conv(0, 0)
            proj(0, 2, 0, 4, bank=py)
            turn_xn(0, 0)
            pe.wait_ge(s_wx, 1)
            token_coef(0, 0)
            turn_conv(0, 1)
            row_coef(0, 0)
            pe.wait_ge(s_sp, 1)
            pe.wait_ge(s_idb, 1)
            pe.wait_ge(s_xrb, 2)
            for n in range(T // 2):
                mm = pe.transpose(pab[:, 128 * n:128 * n + 128],
                                  spread[:, 2 * n:2 * n + 2, :].rearrange("p t j -> p (t j)"), identb[:, :])
            mm.then_inc(s_vt, 1)
            for s in range(AHEAD):
                step_product(0, 0, s)
            pe.wait_ge(s_dd, 1)
            pe.wait_ge(s_later, LATER)
            pair(0, 0)
            pair(1, 1)
            with pe.Fori(MAIN.start, MAIN.stop) as i:
                pair(i)
            pair(14, 14)
            pair(15, 15)
            project_out(15, 0, 2, 4)
            y_group(15, 1, 3)
            turn_y(15, 1)
            project_out(15, 1, 0, 4)

        def conv_sum(eng, i, k):
            eng.wait_ge(s_tap, num(i, k, 1, 1))
            if from_chunk(i, k, 1):
                eng.wait_ge(s_xc, num(i, k))
            eng.tensor_tensor(conv[:, :, :], tap[0][:, :, :], tap[1][:, :, :], ALU.add).then_inc(s_cv, 1)
            for n in range(2, TAPS):
                eng.wait_ge(s_cv, num(i, k, 3, n - 1))
                eng.tensor_tensor(conv[:, :, :], conv[:, :, :], tap[n][:, :, :], ALU.add).then_inc(s_cv, 1)

        def affine(eng, i, k):
            eng.wait_ge(s_xhat, num(i, k, 1, 1))
            if from_chunk(i, k, 2):
                eng.wait_ge(s_scr[k % 2], turn(i, k, 96))
            eng.tensor_tensor(xg[:, :], xhat[:, :], gain[:, :], ALU.mult).then_inc(s_xg, 1)
            eng.wait_ge(s_xg, num(i, k, 1, 1))
            eng.tensor_tensor(xn[k % 2][:, :], xg[:, :], beta[:, :], ALU.add).then_inc(s_xn, 1)

        def residue_1(eng, i, k):
            eng.wait_ge(s_x1, num(i, k, 1, 1))
            if from_chunk(i, k, 1):
                eng.wait_ge(s_x3, num(i, k))
            eng.tensor_tensor(res[:, :], xn[k % 2][:, :], xp[0][k % 2][:, :], ALU.subtract).then_inc(s_r1, 1)

        def part_3(eng, i, k):
            eng.wait_ge(s_x2, num(i, k, 1, 1))
            if from_chunk(i, k, 2):
                eng.wait_ge(s_scr[k % 2], turn(i, k, 96))
            eng.tensor_tensor(xp[2][k % 2][:, :], res[:, :], xp[1][k % 2][:, :], ALU.subtract).then_inc(s_x3, 1)

        def spread_tokens(eng, i, k):
            eng.wait_ge(s_zs, num(i, k, 1, 1))
            if from_chunk(i, k, 1):
                eng.wait_ge(s_blk, num(i, k))
            for n in range(3):
                eng.tensor_tensor(zx[:, n, :, :], bcast(zs[:, NS * n:NS * n + NS], 1, NB),
                                   bcast(tokmask[:, :], 2, NS), ALU.mult).then_inc(s_zx, 1)

        def bd_parts(eng, i, k):
            made, = ready_values(eng, num(i, k, 1, 1))
            eng.wait_ge(*READY)
            eng.wait_ge(s_bc, made)
            eng.tensor_copy(bp[0][:, :], bc[:, 0, :]).then_inc(s_bp, 1)
            eng.wait_ge(s_bp, num(i, k, 4, 1))
            eng.tensor_tensor(bres[:, :], bc[:, 0, :], bp[0][:, :], ALU.subtract).then_inc(s_bp, 1)
            made, = ready_values(eng, num(i, k, 4, 2))
            eng.wait_ge(*READY)
            eng.wait_ge(s_bp, made)
            eng.tensor_copy(bp[1][:, :], bres[:, :]).then_inc(s_bp, 1)
            eng.wait_ge(s_bp, num(i, k, 4, 3))
            eng.tensor_tensor(bp[2][:, :], bres[:, :], bp[1][:, :], ALU.subtract).then_inc(s_bp, 1)

        def spread_rows(eng, i, k):
            eng.wait_ge(s_bp, num(i, k, 4, 4))
            if from_chunk(i, k, 1):
                eng.wait_ge(s_vt, num(i, k))
            for n, p in enumerate(BPART):
                last = eng.tensor_tensor(spread[:, :, NB * n:NB * n + NB], bcast(bp[p][:, :], 2, NB),
                                          bcast(rowmask[:, :], 1, T), ALU.mult)
            last.then_inc(s_sp, 1)
            if from_chunk(i, k, 2):
                eng.wait_ge(s_yg, num(i, k, 4, -4))
            for odd in range(2):
                last = eng.tensor_tensor(
                    cw[k % 2][:, :, 0:128].rearrange("p r (q n) -> p r q n", q=2)[:, :, :, 32 * odd:32 * odd + NB],
                    bcast(bc[:, 1, 8 * odd:8 * odd + 8].rearrange("p (r q) -> p r q", r=4), 3, NB),
                    bcast(bcast(rowmask[:, :], 1, 2), 1, 4), ALU.mult)
            last.then_inc(s_cw, 1)

        @block.vector
        def _(dve):
            def scan_pre(i, k, s):
                if s == 0:
                    dve.wait_ge(s_ad, num(i, k, 1, 1))
                if s >= 1 or from_chunk(i, k, 1):
                    dve.wait_ge(s_h, num(i, k, T, s))
                if s % 2 == 0:
                    dve.wait_ge(s_v, num(i, k, T, s + 2))
                dve.scalar_tensor_tensor(out=pre[:, :], in0=h[:, (s - 1) % 8, :], scalar=ad[k % 2][:, place(s):place(s) + 1],
                                         in1=pv[s % 4][:, :], op0=ALU.mult, op1=ALU.add).then_inc(s_pre, 1)

            def scan_clip(i, k, s):
                dve.wait_ge(s_pre, num(i, k, T, s + 1))
                dve.tensor_scalar(h[:, s % 8, :], pre[:, :], -CLIP, CLIP, ALU.max, ALU.min).then_inc(s_h, 1)

            def norm_stats(i, k, n):
                if n == 0:
                    dve.wait_ge(s_xct, num(i, k, 1, 1))
                    if from_chunk(i, k, 1):
                        dve.wait_ge(s_nmr, num(i, k))
                part = dve.bn_stats(stats[:, n, :], pb[:, 128 * n:128 * n + 128])
                if n == 3:
                    part.then_inc(s_st, 1)

            def norm_mean(i, k):
                made, = ready_values(dve, num(i, k, 2, 1))
                dve.wait_ge(*READY)
                dve.wait_ge(s_st, made)
                dve.bn_aggr(mv[:, :], stats[:, :, :]).then_inc(s_st, 1)

            def norm_cap(i, k):
                dve.wait_ge(s_ss, num(i, k, 1, 1))
                dve.tensor_scalar(sscap[:, :], ss[k % 2][:, :], 1.0, None, ALU.min).then_inc(s_cap, 1)

            def gated(i, k, n):
                cols = slice(128 * n, 128 * n + 128)
                if n == 0:
                    dve.wait_ge(s_yg, num(i, k, 4, 4))
                    dve.wait_ge(s_sg, num(i, k, 1, 1))
                    if from_chunk(i, k, 1):
                        dve.wait_ge(s_yt, num(i, k))
                part = dve.tensor_tensor(yg[:, cols], py[:, cols], sg[:, cols], ALU.mult)
                if n == 3:
                    part.then_inc(s_ygs, 1)

            def pair(i, fixed=None):
                for k in range(2):
                    c = 4 if fixed is None else 2 * fixed + k
                    for s in range(T):
                        scan_pre(i, k, s)
                        scan_clip(i, k, s)
                        if s == 1:
                            if c >= 1:
                                gated(i, k - 1, 0)
                            if c + 1 < NCH:
                                norm_cap(i, k + 1)
                        if s == 2:
                            if c >= 1:
                                gated(i, k - 1, 1)
                        if s == 3:
                            if c >= 1:
                                gated(i, k - 1, 2)
                        if s == 4:
                            if c >= 1:
                                gated(i, k - 1, 3)
                        if s == 5:
                            if c + 2 < NCH:
                                norm_stats(i, k + 2, 0)
                        if s == 6:
                            if c + 2 < NCH:
                                norm_stats(i, k + 2, 1)
                        if s == 7:
                            if c + 2 < NCH:
                                norm_stats(i, k + 2, 2)
                        if s == 8:
                            if c + 2 < NCH:
                                norm_stats(i, k + 2, 3)
                        if s == 9:
                            if c + 2 < NCH:
                                norm_mean(i, k + 2)

            dve.memset(xrb[0][:, :, 0:HIST], 0.0).then_inc(s_zero, 1)
            dve.memset(h[:, 7, :], 0.0).then_inc(s_zero, 1)
            dve.memset(spread[:, :, :], 0.0).then_inc(s_zero, 1)
            for j in range(2):
                dve.memset(cw[j][:, :, :], 0.0).then_inc(s_zero, 1)
            conv_sum(dve, 0, 0)
            dve.wait_ge(s_const, CONST)
            dve.tensor_copy(identb[:, :], ident[:, :]).then_inc(s_idb, 1)
            for m in range(MT):
                part = dve.tensor_scalar(ddiag[:, m, :], ident[:, :], dcol[:, m:m + 1], None, ALU.mult)
            part.then_inc(s_dd, 1)
            dve.wait_ge(s_wdt, 1)
            dve.tensor_copy(wx[:, :, 2 * NS:], pg[:, 0:NS * MT].rearrange("p (m n) -> p m n", m=MT)).then_inc(s_wx, 1)
            for n in range(4):
                norm_stats(0, 0, n)
            norm_mean(0, 0)
            affine(dve, 0, 0)
            residue_1(dve, 0, 0)
            conv_sum(dve, 0, 1)
            norm_cap(0, 0)
            part_3(dve, 0, 0)
            spread_tokens(dve, 0, 0)
            for n in range(4):
                norm_stats(0, 1, n)
            norm_mean(0, 1)
            bd_parts(dve, 0, 0)
            spread_rows(dve, 0, 0)
            affine(dve, 0, 1)
            dve.wait_ge(s_zero, 5)
            pair(0, 0)
            pair(1, 1)
            with dve.Fori(MAIN.start, MAIN.stop) as i:
                pair(i)
            pair(14, 14)
            pair(15, 15)
            for n in range(4):
                gated(15, 1, n)

        @block.scalar
        def _(act):
            def proj_out(i, k, bank=pa):
                act.wait_ge(s_xr, num(i, k, 1, 1))
                product = bank[:, :].rearrange("p (m n) -> p m n", m=MT)
                act.activation(xrb[k % 2][:, :, HIST:], product, ACT.Copy)
                act.activation(xrb[(k + 1) % 2][:, :, 0:HIST], product[:, :, 128 - HIST:], ACT.Copy).then_inc(s_xrb, 1)

            def conv_taps(i, k, first, last):
                if first == 0:
                    act.wait_ge(s_xrb, num(i, k, 1, 1))
                    if from_chunk(i, k, 1):
                        act.wait_ge(s_cv, num(i, k, 3))
                for n in range(first, last):
                    for m in range(MT):
                        a = act.activation(tap[n][:, m, :], xrb[k % 2][:, m, NB * n:NB * n + 128], ACT.Copy,
                                           scale=wconv[:, m, n:n + 1])
                if last == TAPS:
                    a.then_inc(s_tap, 1)

            def conv_silu(i, k):
                act.wait_ge(s_cv, num(i, k, 3, 3))
                if from_chunk(i, k, 2):
                    act.wait_ge(s_xct, num(i, k, 1, -1))
                for m in range(MT):
                    a = act.activation(xc[k % 2][:, m, :].rearrange("p (q r b) -> p q r b", q=4, r=4),
                                       conv[:, m, :].rearrange("p (r q b) -> p q r b", q=4, r=4), ACT.Silu,
                                       bias=bconv[:, m:m + 1])
                a.then_inc(s_xc, 1)

            def normalise(i, k):
                act.wait_ge(s_nmr, num(i, k, 1, 1))
                if from_chunk(i, k, 1):
                    act.wait_ge(s_xg, num(i, k))
                act.activation(xhat[:, :], pb[:, :], ACT.Identity, bias=nmr[:, 0:1], scale=rstd[:, 0:1]
                               ).then_inc(s_xhat, 1)

            def part_1(i, k):
                act.wait_ge(s_xn, num(i, k, 1, 1))
                if from_chunk(i, k, 2):
                    act.wait_ge(s_scr[k % 2], turn(i, k, 96))
                act.activation(xp[0][k % 2][:, :], xn[k % 2][:, :], ACT.Copy).then_inc(s_x1, 1)

            def square(i, k):
                if from_chunk(i, k, 2):
                    act.wait_ge(s_cap, num(i, k, 1, -1))
                act.activation(sq[:, :], xn[k % 2][:, :], ACT.Square, accum_out=ss[k % 2][:, :]).then_inc(s_ss, 1)

            def part_2(i, k):
                act.wait_ge(s_r1, num(i, k, 1, 1))
                act.activation(xp[1][k % 2][:, :], res[:, :], ACT.Copy).then_inc(s_x2, 1)

            def xn_by_channel(i, k):
                act.wait_ge(s_xnt, num(i, k, 1, 1))
                if from_chunk(i, k, 2):
                    act.wait_ge(s_dx, num(i, k, 1, -1))
                act.activation(xnT[k % 2][:, :, :].rearrange("p m n -> p (m n)"), pb[:, :], ACT.Copy).then_inc(s_xnts, 1)

            def token_coef_out(i, k):
                act.wait_ge(s_z, num(i, k, 1, 1))
                act.wait_ge(s_ncap, num(i, k, 1, 1))
                if from_chunk(i, k, 1):
                    act.wait_ge(s_zx, num(i, k, 3))
                act.activation(zs[:, 0:NS], pg[:, 0:NS], ACT.Copy, scale=ncap[:, 0:1])
                act.activation(zs[:, NS:], pg[:, NS:3 * NS], ACT.Copy).then_inc(s_zs, 1)

            def row_coef_out(i, k):
                act.wait_ge(s_blk, num(i, k, 1, 1))
                if from_chunk(i, k, 1):
                    act.wait_ge(s_ad, num(i, k))
                    act.wait_ge(s_cw, num(i, k))
                act.activation(th[:, :], pg[:, BLK + 2 * T:BLK + 3 * T], ACT.Tanh, bias=bdt[:, 0:1]).then_inc(s_th, 1)
                act.activation(bc[:, :, :].rearrange("p n t -> p (n t)"), pg[:, BLK:BLK + 2 * T], ACT.Copy).then_inc(s_bc, 1)

            def bd_parts_out(i, k):
                act.wait_ge(s_vt, num(i, k, 1, 1))
                if from_chunk(i, k, 2):
                    act.wait_ge(s_v, num(i, k, T, -T))
                act.activation(vw[k % 2][:, :, :].rearrange("p n m -> p (n m)"), pab[:, :], ACT.Copy).then_inc(s_vw, 1)

            def gate_silu(i, k):
                act.wait_ge(s_gate, num(i, k, 1, 1))
                if from_chunk(i, k, 1):
                    act.wait_ge(s_ygs, num(i, k))
                act.activation(sg[:, :], pg[:, :], ACT.Silu).then_inc(s_sg, 1)

            def y_by_channel(i, k):
                act.wait_ge(s_yt, num(i, k, 1, 1))
                if from_chunk(i, k, 1):
                    act.wait_ge(s_o, num(i, k))
                act.activation(ygT[:, :, :].rearrange("p m n -> p (m n)"), pb[:, :], ACT.Copy).then_inc(s_yts, 1)

            def output(i, k):
                act.wait_ge(s_o, num(i, k, 1, 1))
                if from_chunk(i, k, 2):
                    act.wait_ge(s_out[k % 2], turn(i, k, 16))
                act.activation(fin[k % 2][:, :], pg[:, OUT], ACT.Copy).then_inc(s_fin, 1)

            def pair(i, fixed=None):
                for k in range(2):
                    c = 4 if fixed is None else 2 * fixed + k
                    if c >= 2:
                        output(i, k - 2)
                    if c + 1 < NCH:
                        xn_by_channel(i, k + 1)
                    if c + 2 < NCH:
                        conv_silu(i, k + 2)
                    if c + 1 < NCH:
                        token_coef_out(i, k + 1)
                        row_coef_out(i, k + 1)
                    if c + 3 < NCH:
                        proj_out(i, k + 3)
                        conv_taps(i, k + 3, 0, 1)
                        conv_taps(i, k + 3, 1, 2)
                    if c + 2 < NCH:
                        normalise(i, k + 2)
                    if c + 1 < NCH:
                        bd_parts_out(i, k + 1)
                    if c + 3 < NCH:
                        conv_taps(i, k + 3, 2, 3)
                    gate_silu(i, k)
                    if c + 2 < NCH:
                        part_1(i, k + 2)
                        square(i, k + 2)
                    if c >= 1:
                        y_by_channel(i, k - 1)
                    if c + 3 < NCH:
                        conv_taps(i, k + 3, 3, TAPS)
                    if c + 2 < NCH:
                        part_2(i, k + 2)

            act.wait_ge(s_zero, 1)
            act.activation(sg[:, 0:HIST], xrb[0][:, 0, 0:HIST], ACT.Silu)
            act.wait_ge(s_first, FIRST)
            proj_out(0, 0)
            conv_taps(0, 0, 0, TAPS)
            act.wait_ge(s_const, CONST)
            act.activation(acol[:, :], alog[:, :], ACT.Tanh).then_inc(s_acol, 1)
            conv_silu(0, 0)
            proj_out(0, 1)
            conv_taps(0, 1, 0, 3)
            normalise(0, 0)
            conv_taps(0, 1, 3, TAPS)
            part_1(0, 0)
            xn_by_channel(0, 0)
            square(0, 0)
            part_2(0, 0)
            proj_out(0, 2, bank=py)
            conv_silu(0, 1)
            token_coef_out(0, 0)
            conv_taps(0, 2, 0, 2)
            row_coef_out(0, 0)
            normalise(0, 1)
            conv_taps(0, 2, 2, 3)
            bd_parts_out(0, 0)
            part_1(0, 1)
            square(0, 1)
            conv_taps(0, 2, 3, TAPS)
            part_2(0, 1)
            pair(0, 0)
            pair(1, 1)
            with act.Fori(MAIN.start, MAIN.stop) as i:
                pair(i)
            pair(14, 14)
            pair(15, 15)
            output(15, 0)
            y_by_channel(15, 1)
            output(15, 1)

        @block.gpsimd
        def _(pool):
            def norm_root(i, k):
                made, = ready_values(pool, num(i, k, 2, 2))
                pool.wait_ge(*READY)
                pool.wait_ge(s_st, made)
                pool.tensor_scalar(vare[:, :], mv[:, 1:2], 1e-5, None, ALU.add).then_inc(s_vare, 1)
                if from_chunk(i, k, 1):
                    pool.wait_ge(s_xhat, num(i, k))
                pool.wait_ge(s_vare, num(i, k, 1, 1))
                pool.tensor_tensor(rstd[:, :], vare[:, :], expo[:, 0:1], ALU.pow).then_inc(s_rstd, 1)
                made, = ready_values(pool, num(i, k, 1, 1))
                pool.wait_ge(*READY)
                pool.wait_ge(s_rstd, made)
                pool.tensor_scalar(nmr[:, :], mv[:, 0:1], rstd[:, 0:1], -1.0, ALU.mult, ALU.mult).then_inc(s_nmr, 1)

            def cap_root(i, k):
                pool.wait_ge(s_cap, num(i, k, 1, 1))
                if from_chunk(i, k, 1):
                    pool.wait_ge(s_zs, num(i, k))
                pool.tensor_tensor(ncap[:, :], sscap[:, :], expo[:, 1:2], ALU.pow).then_inc(s_ncap, 1)

            def decay(i, k):
                made, read = ready_values(pool, num(i, k, 1, 1), num(i, k, T, -T))
                pool.wait_ge(*READY)
                pool.wait_ge(s_th, made)
                if from_chunk(i, k, 2):
                    pool.wait_ge(s_pre, read)
                pool.tensor_scalar(ad[k % 2][:, :], th[:, :], acol[:, 0:1], 1.0, ALU.mult, ALU.add).then_inc(s_ad, 1)

            def pair(i, fixed=None):
                for k in range(2):
                    c = 4 if fixed is None else 2 * fixed + k
                    if c + 1 < NCH:
                        cap_root(i, k + 1)
                    if c >= 1 and c + 1 < NCH:
                        part_3(pool, i, k + 1)
                    if c + 1 < NCH:
                        spread_tokens(pool, i, k + 1)
                        bd_parts(pool, i, k + 1)
                        decay(i, k + 1)
                        spread_rows(pool, i, k + 1)
                    if c + 2 < NCH:
                        norm_root(i, k + 2)
                        affine(pool, i, k + 2)
                        residue_1(pool, i, k + 2)
                    if c + 3 < NCH:
                        conv_sum(pool, i, k + 3)

            pool.wait_ge(s_zero, 5)
            pool.wait_ge(s_const, CONST)
            pool.wait_ge(s_acol, 1)
            pool.tensor_scalar(acol[:, :], acol[:, :], -0.01, None, ALU.mult).then_inc(s_acol, 1)
            pool.wait_ge(s_acol, 2)
            norm_root(0, 0)
            cap_root(0, 0)
            norm_root(0, 1)
            decay(0, 0)
            residue_1(pool, 0, 1)
            conv_sum(pool, 0, 2)
            part_3(pool, 0, 1)
            pair(0, 0)
            pair(1, 1)
            with pool.Fori(MAIN.start, MAIN.stop) as i:
                pair(i)
            pair(14, 14)
            pair(15, 15)


def host_layout(a):
    def turned(w, tiles):
        return np.ascontiguousarray(w.T.reshape(tiles, 128, w.shape[0]).transpose(1, 0, 2))

    def per_channel(w):
        return np.ascontiguousarray(w.reshape(MT, 128, -1).transpose(1, 0, 2))

    def on_all(v):
        return np.ascontiguousarray(np.broadcast_to(v[None, :], (128, v.shape[0])))

    def on_rows(v):
        return np.ascontiguousarray(np.broadcast_to(v[None, :], (NB, NS)).reshape(128, 1))

    x = a["x"].reshape(NB, NCH, 4, 4, DM).transpose(1, 3, 2, 0, 4)
    xT = np.ascontiguousarray(x.reshape(NCH, 128, KT, 128).transpose(0, 3, 2, 1))
    p = np.arange(128)
    column = 2 * (p // 8 % 8) + p // 64
    f = np.float32
    pre = "L0_cond_"
    return {
        "xT": xT, "w_in": turned(a[pre + "W_in"], KT), "w_out": turned(a[pre + "W_out"], MT),
        "w_xp": turned(a[pre + "W_xproj"], MT), "w_xdt": np.ascontiguousarray(a[pre + "W_xproj"][2 * NS:]),
        "w_dt": np.ascontiguousarray(a[pre + "W_dt"].T), "cond": np.ascontiguousarray(a["cond_2048"]),
        "ind8": (p[None, :] % NB == np.arange(NB)[:, None]).astype(f),
        "w_conv": per_channel(a[pre + "W_conv"]), "b_conv": per_channel(a[pre + "b_conv"])[:, :, 0].copy(),
        "gain": on_all(a[pre + "ln_g"]), "beta": on_all(a[pre + "ln_b"]), "dcol": per_channel(a[pre + "D"])[:, :, 0].copy(),
        "alog": on_rows(a[pre + "A_log"]), "b_dt": on_rows(a[pre + "b_dt"]), "ident": np.eye(128, dtype=f),
        "rowmask": (p[:, None] // NS == np.arange(NB)[None, :]).astype(f),
        "tokmask": (p[:, None] % NB == np.arange(NB)[None, :]).astype(f),
        "tsel": (column[:, None] == np.arange(T)[None, :]).astype(f),
        "expo": np.ascontiguousarray(np.broadcast_to(np.array([-0.5, 0.5], f), (128, 2))),
    }


def declare(nc, arrays):
    d = {n: nc.dram_tensor(f"in_{n}", v.shape, F32, kind="ExternalInput").ap() for n, v in arrays.items()}
    d["out"] = nc.dram_tensor("out_0", (NCH, 128, DM), F32, kind="ExternalOutput").ap()
    return d


def kernel(**inputs):
    import concourse.bacc as _bacc
    from concourse.bass_utils import run_bass_kernel_spmd as run

    arrays = host_layout({k: np.asarray(v) for k, v in inputs.items()})
    nc = _bacc.Bacc("TRN2", target_bir_lowering=False, num_devices=1)
    build(nc, declare(nc, arrays))
    r = run(nc, [{f"in_{n}": v for n, v in arrays.items()}], core_ids=[0])
    out = r.results[0]["out_0"].reshape(NCH, 4, 4, NB, DM)
    return np.ascontiguousarray(out.transpose(3, 0, 2, 1, 4).reshape(NB, SEQ, DM))
```
